# Optimizing a Trainium2 kernel written in Bass

```python
import numpy as np
import jax
import jax.numpy as jnp

def _softmax(x, axis=-1):
    return jax.nn.softmax(x, axis=axis)

def _gelu(x):
    return jax.nn.gelu(x, approximate=True)

def _silu(x):
    return jax.nn.silu(x)

def _sigmoid(x):
    return jax.nn.sigmoid(x)

def _layernorm(x, axis=-1, eps=1e-05):
    m = jnp.mean(x, axis=axis, keepdims=True)
    v = jnp.var(x, axis=axis, keepdims=True)
    return (x - m) / jnp.sqrt(v + eps)

def _scatter_add(tgt, idx, src, axis=0):
    return tgt.at[idx].add(src)

def _segment_sum(src, seg, n):
    return jax.ops.segment_sum(src, seg, n)
kernel_name = 'mk_prb_d1_jaxref_r8_5249ec'

def setup_inputs(seed: int=0):
    np.random.seed(seed)
    _w = jnp.asarray

    def _L0_attn_setup():
        import jax, jax.numpy as jnp
        import numpy as np
        N_EMBD = 128
        BLOCK_SIZE = 256
        ATTN_SPAN = 32
        LN_EPS = 1e-05

        def _band_mask(T, span, dtype):
            ones = jnp.ones((T, T), dtype=dtype)
            return jnp.tril(ones, 0) * (1.0 - jnp.tril(ones, -span))

        def _layer_norm(h, w, b):
            mu = jnp.mean(h, axis=-1, keepdims=True)
            var = jnp.var(h, axis=-1, keepdims=True)
            return (h - mu) * jax.lax.rsqrt(var + LN_EPS) * w + b
        key = jax.random.key(seed)
        k_x, k_w, k_b, k_lw = jax.random.split(key, 4)
        B, T, C = (4, BLOCK_SIZE, N_EMBD)
        x = jax.random.normal(k_x, (B, T, C), dtype=jnp.float32)
        lim = 1.0 / np.sqrt(C)
        W_qkv = jax.random.uniform(k_w, (C, 3 * C), minval=-lim, maxval=lim, dtype=jnp.float32)
        b_qkv = jax.random.uniform(k_b, (3 * C,), minval=-lim, maxval=lim, dtype=jnp.float32)
        ln_w = jnp.ones((C,), dtype=jnp.float32)
        ln_b = jnp.zeros((C,), dtype=jnp.float32)
        return {'x': x, 'W_qkv': W_qkv, 'b_qkv': b_qkv, 'ln_w': ln_w, 'ln_b': ln_b}
    _L0_attn_in = _L0_attn_setup()

    def _L0_ffn_setup():
        import jax, jax.numpy as jnp
        import numpy as np
        INT4_QMAX = 7.0

        def simulate_quantize_int4(w):
            scale = jnp.max(jnp.abs(w)) / INT4_QMAX
            q = jnp.clip(jnp.round(w / scale), -8.0, 7.0)
            return q * scale
        key = jax.random.key(seed)
        k_x, k_w, k_bias, k_a, k_b = jax.random.split(key, 5)
        d_in, features, rank = (128, 128, 16)
        x = jax.random.normal(k_x, (4, 1024, d_in), dtype=jnp.float32)
        kernel = jax.random.normal(k_w, (d_in, features), dtype=jnp.float32)
        bias = jax.random.normal(k_bias, (features,), dtype=jnp.float32)
        a = jax.random.normal(k_a, (d_in, rank), dtype=jnp.float32) * (1.0 / np.sqrt(d_in))
        b = jax.random.normal(k_b, (rank, features), dtype=jnp.float32) * 0.01
        return {'x': x, 'kernel': kernel, 'bias': bias, 'a': a, 'b': b}
    _L0_ffn_in = _L0_ffn_setup()
    _d = {'L0_attn_x': _L0_attn_in['x'], 'L0_attn_W_qkv': _L0_attn_in['W_qkv'], 'L0_attn_b_qkv': _L0_attn_in['b_qkv'], 'L0_attn_ln_w': _L0_attn_in['ln_w'], 'L0_attn_ln_b': _L0_attn_in['ln_b'], 'L0_ffn_kernel': _L0_ffn_in['kernel'], 'L0_ffn_bias': _L0_ffn_in['bias'], 'L0_ffn_a': _L0_ffn_in['a'], 'L0_ffn_b': _L0_ffn_in['b']}
    _x0 = _d['L0_attn_x']
    _d['L0_attn_x'] = jax.random.normal(jax.random.fold_in(jax.random.key(seed), 1), (4, 1024, 128), dtype=_x0.dtype)
    del _x0
    return _d

def reference(L0_attn_x, L0_attn_W_qkv, L0_attn_b_qkv, L0_attn_ln_w, L0_attn_ln_b, L0_ffn_kernel, L0_ffn_bias, L0_ffn_a, L0_ffn_b):

    def _L0_attn_ref(x, W_qkv, b_qkv, ln_w, ln_b):
        import jax, jax.numpy as jnp
        import numpy as np
        N_EMBD = 128
        BLOCK_SIZE = 256
        ATTN_SPAN = 32
        LN_EPS = 1e-05

        def _band_mask(T, span, dtype):
            ones = jnp.ones((T, T), dtype=dtype)
            return jnp.tril(ones, 0) * (1.0 - jnp.tril(ones, -span))

        def _layer_norm(h, w, b):
            mu = jnp.mean(h, axis=-1, keepdims=True)
            var = jnp.var(h, axis=-1, keepdims=True)
            return (h - mu) * jax.lax.rsqrt(var + LN_EPS) * w + b
        B, T, C = x.shape
        qkv = x @ W_qkv + b_qkv
        q, k, v = jnp.split(qkv, 3, axis=-1)
        scale = np.sqrt(C * ATTN_SPAN).astype(np.float32)
        scores = jnp.einsum('bid,bjd->bij', q, k) / scale
        scores = scores * _band_mask(T, ATTN_SPAN, x.dtype)[None, :, :]
        out = jnp.einsum('bij,bjd->bid', scores, v)
        return _layer_norm(out, ln_w, ln_b)

    def _L0_ffn_ref(x, kernel, bias, a, b):
        import jax, jax.numpy as jnp
        import numpy as np
        INT4_QMAX = 7.0

        def simulate_quantize_int4(w):
            scale = jnp.max(jnp.abs(w)) / INT4_QMAX
            q = jnp.clip(jnp.round(w / scale), -8.0, 7.0)
            return q * scale
        w = simulate_quantize_int4(kernel)
        y = jnp.einsum('bsd,df->bsf', x, w) + bias
        lora = jnp.einsum('bsr,rf->bsf', jnp.einsum('bsd,dr->bsr', x, a), b)
        return y + lora
    x = L0_attn_x
    xn = _layernorm(x, axis=-1)
    x = x + _L0_attn_ref(xn, L0_attn_W_qkv, L0_attn_b_qkv, L0_attn_ln_w, L0_attn_ln_b) + _L0_ffn_ref(xn, L0_ffn_kernel, L0_ffn_bias, L0_ffn_a, L0_ffn_b)
    return x

_drawn_inputs = setup_inputs


def setup_inputs(seed=0):
    import zlib

    import numpy as np

    out = dict(_drawn_inputs(seed))
    spreads = {'L0_attn_ln_w': (1.0, 0.6), 'L0_attn_ln_b': (0.0, 0.8)}
    factors = {'L0_attn_b_qkv': 4.042, 'L0_ffn_a': 8.0, 'L0_ffn_b': 8.0}
    for name, (base, spread) in spreads.items():
        noise = np.random.default_rng([zlib.crc32(name.encode()), seed]).standard_normal(out[name].shape)
        drawn = base * np.exp(spread * noise) if base else spread * noise
        out[name] = jnp.asarray(drawn.astype(out[name].dtype))
    for name, factor in factors.items():
        out[name] = (out[name] * factor).astype(out[name].dtype)
    return out
```

```python
import concourse.bass as bass
from concourse import mybir
from contextlib import ExitStack

F32 = mybir.dt.float32
I32 = mybir.dt.int32
ALU = mybir.AluOpType
ACT = mybir.ActivationFunctionType
AX = mybir.AxisListType


def band_block_kernel(nc, x, w_qkv, b_qkv, ln_w, ln_b, w_ffn, bias_ffn, lora_a, lora_b, out):
    C = 128
    B, T, _ = x.shape
    TILES = 4
    UTOK = TILES * C
    HEAD = 2
    UNITS = T // UTOK
    SPAN = 32
    REACH = C + SPAN
    HALF = C // 2
    RANK = lora_a.shape[1]
    EPS = 1e-5
    SCORE_SCALE = 1.0 / float(C * SPAN) ** 0.5
    QMAX = 7.0
    ROUND = 12582912.0
    TOP12 = -4096
    assert UNITS == 2 and x.shape[2] == C

    x_v = x.rearrange("b (u k p) c -> b u p k c", u=UNITS, p=C)
    out_v = out.rearrange("b (u k p) c -> b u p k c", u=UNITS, p=C)

    with ExitStack() as ctx:
        def sb(name, shape, dt=F32):
            return ctx.enter_context(nc.sbuf_tensor(name, shape, dt))

        def pb(name, shape=(128, 512)):
            return ctx.enter_context(nc.psum_tensor(name, list(shape), F32))

        def sem(name):
            return ctx.enter_context(nc.semaphore(name))

        wqkv_sb = sb("wqkv_sb", [C, 3 * C])
        bqk_col = sb("bqk_col", [C, 2])
        bv_row = sb("bv_row", [1, C])
        bias_rows = sb("bias_rows", [2, C])
        wf_raw = sb("wf_raw", [C, C])
        a_sb = sb("a_sb", [C, RANK])
        b_sb = sb("b_sb", [RANK, C])
        lnw_b = sb("lnw_b", [C, C])
        ident = sb("ident", [C, C])
        centre = sb("centre", [C, C])
        ones = sb("ones", [C, C])
        inv_rows = sb("inv_rows", [2, C])
        mask = sb("mask", [C, REACH])
        minus_half = sb("minus_half", [C, TILES])
        eps_col = sb("eps_col", [C, TILES])
        bqk_c = sb("bqk_c", [C, 2])
        wsum = sb("wsum", [C, 4])
        wcoef = sb("wcoef", [C, 4])
        wjunk = sb("wjunk", [C, 4, C])
        wqT = sb("wqT", [C, C])
        wkT = sb("wkT", [C, C])
        g_sb = sb("g_sb", [C, C])
        wv_sb = sb("wv_sb", [C, C])
        aT_sb = sb("aT_sb", [RANK, C])
        wf_sb = sb("wf_sb", [C, C])
        small = sb("small", [C, 12])
        amax, gmax, q0, e7a, e7, scale, rscale, nrscale, sc_hi, sc_lo = (small[:, n:n + 1] for n in range(10))
        dmax = sb("dmax", [C, C])
        quo = sb("quo", [C, C])
        quo_hi = sb("quo_hi", [C, C])
        quo_lo = sb("quo_lo", [C, C])
        res = sb("res", [C, 4, C])
        quo2 = sb("quo2", [C, C])
        qint = sb("qint", [C, C])
        qclip = sb("qclip", [C, C])
        wq4 = sb("wq4", [C, C])
        x_sb = sb("x_sb", [C, B * UNITS * TILES, C])
        stats = [sb(f"stats{h}", [C, TILES, 6]) for h in range(2)]
        sdiff = [sb(f"sdiff{h}", [C, TILES]) for h in range(2)]
        ssum = [sb(f"ssum{h}", [C, TILES]) for h in range(2)]
        var_even = [sb(f"var_even{h}", [C, TILES]) for h in range(2)]
        var_both = [sb(f"var_both{h}", [C, TILES]) for h in range(2)]
        var_diff = [sb(f"var_diff{h}", [C, TILES]) for h in range(2)]
        vareps = [sb(f"vareps{h}", [C, TILES]) for h in range(2)]
        rstd = [sb(f"rstd{h}", [C, TILES]) for h in range(2)]
        mr = [sb(f"mr{h}", [C, TILES]) for h in range(2)]
        shift = [sb(f"shift{h}", [C, TILES]) for h in range(2)]
        xt = [sb(f"xt{h}", [C, TILES, C]) for h in range(2)]
        xt_carry = sb("xt_carry", [C, C])
        xtT = [sb(f"xtT{h}", [C, UTOK]) for h in range(2)]
        zT = [sb(f"zT{h}", [C, UTOK]) for h in range(2)]
        sm = [sb(f"sm{h}", [C, TILES, REACH]) for h in range(2)]
        sxT = [sb(f"sxT{h}", [C, UTOK]) for h in range(2)]
        sq_junk = sb("sq_junk", [C, TILES, C])
        ssq = [sb(f"ssq{h}", [C, TILES]) for h in range(2)]
        vareps2 = [sb(f"vareps2{h}", [C, TILES]) for h in range(2)]
        rstd2 = [sb(f"rstd2{h}", [C, TILES]) for h in range(2)]
        att = [sb(f"att{h}", [C, TILES, C]) for h in range(2)]
        xy = [sb(f"xy{h}", [C, TILES, C]) for h in range(2)]
        res_out = [sb(f"res_out{h}", [C, TILES, C]) for h in range(2)]

        w_ps = pb("w_ps")
        xT_ps = pb("xT_ps")
        z_ps = pb("z_ps")
        s_ps = [pb(f"s_ps{n}") for n in range(2)]
        sx_ps = pb("sx_ps")
        o_ps = pb("o_ps")
        y_ps = pb("y_ps")

        wqkv_in, bqk_in, bv_in, biasf_in, lnb_in, wf_in, a_in, b_in, lnw_in = (
            sem(n) for n in ("wqkv_in", "bqk_in", "bv_in", "biasf_in", "lnb_in", "wf_in", "a_in", "b_in", "lnw_in"))
        x_in = [sem(f"x_in{h}") for h in range(2)]
        stored = [sem(f"stored{h}") for h in range(2)]
        ident_set = sem("ident_set")
        consts_set = sem("consts_set")
        pool_chain = sem("pool_chain")
        s_ps_zeroed = sem("s_ps_zeroed")
        qkT_done = sem("qkT_done")
        aT_done = sem("aT_done")
        act_chain = sem("act_chain")
        qk_ready = sem("qk_ready")
        aT_ready = sem("aT_ready")
        g_done = sem("g_done")
        g_ready = sem("g_ready")
        wv_done = sem("wv_done")
        wv_ready = sem("wv_ready")
        dmax_ready = sem("dmax_ready")
        gmax_done = sem("gmax_done")
        dve_chain = sem("dve_chain")
        wq4_ready = sem("wq4_ready")
        wf_done = sem("wf_done")
        wf_ready = sem("wf_ready")
        bn_done = sem("bn_done")
        stats_ready = sem("stats_ready")
        stats_chain = sem("stats_chain")
        rstd_ready = sem("rstd_ready")
        shift_chain = sem("shift_chain")
        shift_ready = sem("shift_ready")
        xt_head_ready = sem("xt_head_ready")
        xt_tail_ready = sem("xt_tail_ready")
        carry_ready = sem("carry_ready")
        xT_done = sem("xT_done")
        xtT_ready = sem("xtT_ready")
        z_done = sem("z_done")
        zT_ready = sem("zT_ready")
        s_done = sem("s_done")
        sm_ready = sem("sm_ready")
        sx_done = sem("sx_done")
        sxT_ready = sem("sxT_ready")
        o_done = sem("o_done")
        ssq_ready = sem("ssq_ready")
        rstd2_chain = sem("rstd2_chain")
        rstd2_ready = sem("rstd2_ready")
        att_ready = sem("att_ready")
        y_done = sem("y_done")
        xy_ready = sem("xy_ready")
        res_ready = [sem(f"res_ready{h}") for h in range(2)]

        def unit_of_x(i, h, k, count=1):
            first = (2 * i + h) * TILES + k
            if isinstance(first, int):
                return x_sb[:, first:first + count, :]
            return x_sb[:, bass.ds(first, count), :]

        block = ctx.enter_context(nc.Block())

        @block.sync
        def _(sp):
            for h in range(UNITS):
                sp.sem_inc(stored[h], 16)
            for h in range(UNITS):
                sp.dma_start(x_sb[:, h * TILES:(h + 1) * TILES, :], x_v[0, h]).then_inc(x_in[h], 16)
            with sp.Fori(1, B) as i:
                for h in range(UNITS):
                    sp.wait_ge(x_in[h], 16 * i)
                    sp.dma_start(x_sb[:, bass.ds((2 * i + h) * TILES, TILES), :], x_v[i, h]).then_inc(x_in[h], 16)
            with sp.Fori(0, B) as i:
                for h in range(UNITS):
                    sp.wait_ge(res_ready[h], i + 1)
                    sp.dma_start(out_v[i, h], res_out[h][:, :, :]).then_inc(stored[h], 16)
            for h in range(UNITS):
                sp.wait_ge(stored[h], 16 * (B + 1))

        @block.gpsimd
        def _(pool):
            nc.gpsimd.memset(ident[:, :], 0.0).then_inc(pool_chain, 1)
            nc.gpsimd.memset(ones[:, :], 1.0)
            nc.gpsimd.memset(minus_half[:, :], -0.5)
            nc.gpsimd.memset(eps_col[:, :], EPS)
            nc.gpsimd.memset(inv_rows[:, :], 1.0 / C)
            nc.gpsimd.memset(centre[:, :], -1.0 / C).then_inc(pool_chain, 1)
            nc.gpsimd.memset(mask[:, :], 1.0).then_inc(pool_chain, 1)
            pool.wait_ge(pool_chain, 3)
            nc.gpsimd.affine_select(out=ident[:, :], in_=ident[:, :], compare_op=ALU.not_equal, fill=1.0,
                                    base=0, pattern=[[-1, C]], channel_multiplier=1).then_inc(ident_set, 1)
            nc.gpsimd.affine_select(out=centre[:, :], in_=centre[:, :], compare_op=ALU.not_equal,
                                    fill=1.0 - 1.0 / C, base=0, pattern=[[-1, C]], channel_multiplier=1)
            nc.gpsimd.affine_select(out=mask[:, :], in_=mask[:, :], compare_op=ALU.is_ge, fill=0.0,
                                    base=0, pattern=[[1, REACH]], channel_multiplier=-1).then_inc(pool_chain, 1)
            pool.wait_ge(pool_chain, 4)
            nc.gpsimd.affine_select(out=mask[:, :], in_=mask[:, :], compare_op=ALU.is_ge, fill=0.0,
                                    base=SPAN - 1, pattern=[[-1, REACH]],
                                    channel_multiplier=1).then_inc(consts_set, 1)

            def inverse_deviation(i, h):
                u = 2 * i + h
                pool.wait_ge(stats_ready, u + 1)
                if not isinstance(u, int) or u >= 2:
                    pool.wait_ge(xt_head_ready, u - 1)
                nc.gpsimd.tensor_tensor(rstd[h][:, :], vareps[h][:, :], minus_half[:, :],
                                        ALU.pow).then_inc(rstd_ready, 1)

            def second_norm(i, h):
                u = 2 * i + h
                pool.wait_ge(ssq_ready, u + 1)
                nc.gpsimd.tensor_tensor(vareps2[h][:, :], ssq[h][:, :], eps_col[:, :],
                                        ALU.add).then_inc(rstd2_chain, 1)
                pool.wait_ge(rstd2_chain, u + 1)
                nc.gpsimd.tensor_tensor(rstd2[h][:, :], vareps2[h][:, :], minus_half[:, :],
                                        ALU.pow).then_inc(rstd2_ready, 1)

            def finish(i, h):
                u = 2 * i + h
                pool.wait_ge(att_ready, u + 1)
                pool.wait_ge(xy_ready, u + 1)
                pool.wait_ge(stored[h], 16 * (i + 1))
                nc.gpsimd.tensor_tensor(res_out[h][:, :, :], att[h][:, :, :], xy[h][:, :, :],
                                        ALU.add).then_inc(res_ready[h], 1)

            for u in range(3):
                inverse_deviation(u // 2, u % 2)
            with pool.Fori(0, B - 2) as i:
                for h in range(UNITS):
                    inverse_deviation(*((i + 1, 1), (i + 2, 0))[h])
                    second_norm(i, h)
                    finish(i, h)
            inverse_deviation(B - 1, 1)
            for u in range(2 * (B - 2), 2 * B):
                second_norm(u // 2, u % 2)
                finish(u // 2, u % 2)

        @block.scalar
        def _(act):
            act.dma_start(wqkv_sb[:, :], w_qkv).then_inc(wqkv_in, 16)
            act.dma_start(wf_raw[:, :], w_ffn).then_inc(wf_in, 16)
            act.dma_start(bqk_col[:, :], b_qkv[0:2 * C].rearrange("(n p) -> p n", p=C),
                          allow_slow_non_contiguous=True).then_inc(bqk_in, 16)
            act.dma_start(a_sb[:, :], lora_a).then_inc(a_in, 16)
            act.dma_start(b_sb[:, :], lora_b).then_inc(b_in, 16)
            act.dma_start(bv_row[:, :], b_qkv[2 * C:3 * C].rearrange("(a n) -> a n", a=1)).then_inc(bv_in, 16)
            act.dma_start(bias_rows[0:1, :], bias_ffn.rearrange("(a n) -> a n", a=1)).then_inc(biasf_in, 16)
            act.dma_start(bias_rows[1:2, :], ln_b.rearrange("(a n) -> a n", a=1)).then_inc(lnb_in, 16)
            act.dma_start(lnw_b[:, :], ln_w.rearrange("(a n) -> a n", a=1).to_broadcast([C, C])).then_inc(lnw_in, 16)

            act.wait_ge(bqk_in, 16)
            nc.scalar.activation(bqk_c[:, :], bqk_col[:, :], ACT.Copy, scale=1.0 / C)
            act.wait_ge(qkT_done, 1)
            for n in range(2):
                nc.scalar.activation(wjunk[:, n, :], w_ps[:, n * C:(n + 1) * C], ACT.Copy,
                                     accum_out=wsum[:, n:n + 1]).then_inc(act_chain, 1)
            act.wait_ge(act_chain, 2)
            for n in range(2):
                nc.scalar.activation(wcoef[:, n:n + 1], wsum[:, n:n + 1], ACT.Identity, scale=-1.0 / C,
                                     bias=bqk_c[:, n:n + 1]).then_inc(act_chain, 1)
            act.wait_ge(act_chain, 4)
            for n, dst in enumerate((wqT, wkT)):
                nc.scalar.activation(dst[:, :], w_ps[:, n * C:(n + 1) * C], ACT.Identity,
                                     bias=wcoef[:, n:n + 1]).then_inc(qk_ready, 1)

            def evacuate_xT(i, h):
                act.wait_ge(xT_done, 2 * i + h + 1)
                nc.scalar.activation(xtT[h][:, :], xT_ps[:, :], ACT.Copy).then_inc(xtT_ready, 1)

            def evacuate_z(i, h):
                act.wait_ge(z_done, 2 * i + h + 1)
                nc.scalar.activation(zT[h][:, :], z_ps[:, :], ACT.Copy).then_inc(zT_ready, 1)

            def evacuate_sx(i, h):
                act.wait_ge(sx_done, 2 * i + h + 1)
                nc.scalar.activation(sxT[h][:, :], sx_ps[:, :], ACT.Copy).then_inc(sxT_ready, 1)

            def square_sums(i, h):
                act.wait_ge(o_done, 2 * i + h + 1)
                for k in range(TILES):
                    last = nc.scalar.activation(sq_junk[:, k, :], o_ps[:, k * C:(k + 1) * C], ACT.Square,
                                                scale=float(C) ** -0.5,
                                                accum_out=ssq[h][:, k:k + 1])
                last.then_inc(ssq_ready, 1)

            def keep_carry(i):
                act.wait_ge(xt_tail_ready, 2 * i + 1)
                if not isinstance(i, int) or i > 0:
                    act.wait_ge(sx_done, 2 * i)
                nc.scalar.activation(xt_carry[:, :], xt[0][:, TILES - 1, :], ACT.Copy).then_inc(carry_ready, 1)

            def normalise(i, h, k):
                if k == 0:
                    act.wait_ge(shift_ready, 2 * i + h + 1)
                ins = nc.scalar.activation(xt[h][:, k:k + 1, :], unit_of_x(i, h, k), ACT.Identity,
                                           scale=rstd[h][:, k:k + 1], bias=shift[h][:, k:k + 1])
                if k == HEAD - 1:
                    ins.then_inc(xt_head_ready, 1)

            for k in range(HEAD):
                normalise(0, 0, k)
            act.wait_ge(g_done, 1)
            nc.scalar.activation(g_sb[:, :], z_ps[:, 0:C], ACT.Copy, scale=SCORE_SCALE).then_inc(g_ready, 1)
            evacuate_xT(0, 0)
            act.wait_ge(aT_done, 1)
            nc.scalar.activation(wjunk[0:RANK, 2, :], y_ps[0:RANK, 0:C], ACT.Copy,
                                 accum_out=wsum[0:RANK, 2:3]).then_inc(act_chain, 1)
            act.wait_ge(act_chain, 5)
            nc.scalar.activation(wcoef[0:RANK, 2:3], wsum[0:RANK, 2:3], ACT.Copy,
                                 scale=-1.0 / C).then_inc(act_chain, 1)
            act.wait_ge(act_chain, 6)
            nc.scalar.activation(aT_sb[:, :], y_ps[0:RANK, 0:C], ACT.Identity,
                                 bias=wcoef[0:RANK, 2:3]).then_inc(aT_ready, 1)
            evacuate_z(0, 0)
            act.wait_ge(wv_done, 1)
            nc.scalar.activation(wjunk[:, 3, :], o_ps[:, 0:C], ACT.Copy,
                                 accum_out=wsum[:, 3:4]).then_inc(act_chain, 1)
            act.wait_ge(act_chain, 7)
            nc.scalar.activation(wcoef[:, 3:4], wsum[:, 3:4], ACT.Copy, scale=-1.0 / C).then_inc(act_chain, 1)
            act.wait_ge(act_chain, 8)
            nc.scalar.activation(wv_sb[:, :], o_ps[:, 0:C], ACT.Identity,
                                 bias=wcoef[:, 3:4]).then_inc(wv_ready, 1)

            def step(i, h, following, second):
                if following:
                    evacuate_xT(*following)
                evacuate_sx(i, h)
                if second:
                    normalise(*second, 0)
                if following:
                    evacuate_z(*following)
                if second:
                    normalise(*second, 1)
                if h and following:
                    keep_carry(i + 1)
                square_sums(i, h)

            keep_carry(0)
            for k in range(HEAD):
                normalise(0, 1, k)
            evacuate_xT(0, 1)
            evacuate_sx(0, 0)
            normalise(1, 0, 0)
            evacuate_z(0, 1)
            normalise(1, 0, 1)
            square_sums(0, 0)
            act.wait_ge(wf_done, 1)
            nc.scalar.activation(wf_sb[:, :], w_ps[:, 0:C], ACT.Copy).then_inc(wf_ready, 1)
            with act.Fori(0, B - 2) as i:
                step(i, 1, (i + 1, 0), (i + 1, 1))
                step(i + 1, 0, (i + 1, 1), (i + 2, 0))
            step(B - 2, 1, (B - 1, 0), (B - 1, 1))
            step(B - 1, 0, (B - 1, 1), None)
            step(B - 1, 1, None, None)

        @block.vector
        def _(dve):
            def link(count, ins):
                ins.then_inc(dve_chain, 1)
                dve.wait_ge(dve_chain, count)

            def statistics(i, h):
                u = 2 * i + h
                dve.wait_ge(x_in[h], 16 * (i + 1))
                for k in range(TILES):
                    last = nc.vector.bn_stats(stats[h][:, k, :], unit_of_x(i, h, k))
                last.then_inc(bn_done, 1)
                dve.wait_ge(bn_done, u + 1)
                st = stats[h]
                nc.vector.tensor_tensor(sdiff[h][:, :], st[:, :, 1], st[:, :, 4], ALU.subtract)
                nc.vector.tensor_scalar(var_even[h][:, :], st[:, :, 2], 1.0 / C, EPS,
                                        ALU.mult, ALU.add).then_inc(stats_chain, 1)
                nc.vector.tensor_tensor(ssum[h][:, :], st[:, :, 1], st[:, :, 4], ALU.add)
                dve.wait_ge(stats_chain, 2 * u + 1)
                nc.vector.scalar_tensor_tensor(var_diff[h][:, :], sdiff[h][:, :], 0.25, sdiff[h][:, :],
                                               ALU.mult, ALU.mult)
                nc.vector.scalar_tensor_tensor(var_both[h][:, :], st[:, :, 5], 1.0 / C, var_even[h][:, :],
                                               ALU.mult, ALU.add).then_inc(stats_chain, 1)
                dve.wait_ge(stats_chain, 2 * u + 2)
                nc.vector.tensor_tensor(vareps[h][:, :], var_both[h][:, :], var_diff[h][:, :],
                                        ALU.add).then_inc(stats_ready, 1)

            def normalise(i, h):
                u = 2 * i + h
                dve.wait_ge(rstd_ready, u + 1)
                nc.vector.scalar_tensor_tensor(mr[h][:, :], ssum[h][:, :], -0.5, rstd[h][:, :],
                                               ALU.mult, ALU.mult).then_inc(shift_chain, 1)
                dve.wait_ge(shift_chain, u + 1)
                nc.vector.tensor_scalar(shift[h][:, :], mr[h][:, :], 1.0, None, ALU.add).then_inc(shift_ready, 1)
                if not isinstance(u, int) or u >= 2:
                    dve.wait_ge(sx_done, u - 1)
                    if h == 0:
                        dve.wait_ge(carry_ready, i)
                dve.wait_ge(shift_ready, u + 1)
                for k in range(HEAD, TILES):
                    last = nc.vector.tensor_scalar(xt[h][:, k:k + 1, :], unit_of_x(i, h, k), rstd[h][:, k:k + 1],
                                                   shift[h][:, k:k + 1], ALU.mult, ALU.add)
                last.then_inc(xt_tail_ready, 1)

            def mask_scores(i, h):
                for n in range(2):
                    dve.wait_ge(s_done, 2 * (2 * i + h) + n + 1)
                    nc.vector.tensor_tensor(
                        sm[h][:, 2 * n:2 * n + 2, :],
                        s_ps[n][:, 0:2 * REACH].rearrange("p (k r) -> p k r", k=2),
                        mask[:, :].unsqueeze(1).to_broadcast([C, 2, REACH]), ALU.mult).then_inc(sm_ready, 1)

            def add_residual(i, h):
                dve.wait_ge(y_done, 2 * i + h + 1)
                nc.vector.tensor_tensor(xy[h][:, :, :], y_ps[:, :].rearrange("p (k c) -> p k c", k=TILES),
                                        unit_of_x(i, h, 0, TILES), ALU.add).then_inc(xy_ready, 1)

            def second_norm(i, h):
                dve.wait_ge(rstd2_ready, 2 * i + h + 1)
                for k in range(TILES):
                    last = nc.vector.scalar_tensor_tensor(att[h][:, k, :], o_ps[:, k * C:(k + 1) * C],
                                                          rstd2[h][:, k:k + 1], lnw_b[:, :], ALU.mult, ALU.mult)
                last.then_inc(att_ready, 1)

            nc.vector.memset(s_ps[0][:, :], 0.0)
            nc.vector.memset(s_ps[1][:, :], 0.0).then_inc(s_ps_zeroed, 1)
            statistics(0, 0)
            dve.wait_ge(wf_in, 16)
            link(1, nc.vector.tensor_reduce(amax, wf_raw[:, :], AX.X, ALU.max, apply_absolute_value=True))
            dve.wait_ge(ident_set, 1)
            nc.vector.tensor_scalar(dmax[:, :], ident[:, :], amax, None, ALU.mult).then_inc(dmax_ready, 1)
            statistics(0, 1)
            normalise(0, 0)
            dve.wait_ge(gmax_done, 1)
            link(2, nc.vector.tensor_reduce(gmax, sx_ps[:, 0:C], AX.X, ALU.max))
            link(3, nc.vector.tensor_scalar(q0, gmax, 1.0 / QMAX, None, ALU.mult))
            link(4, nc.vector.scalar_tensor_tensor(e7a, q0, -(QMAX + 1.0), gmax, ALU.mult, ALU.add))
            link(5, nc.vector.tensor_tensor(e7, e7a, q0, ALU.add))
            link(6, nc.vector.scalar_tensor_tensor(scale, e7, 1.0 / QMAX, q0, ALU.mult, ALU.add))
            link(7, nc.vector.reciprocal(rscale, scale))
            nc.vector.tensor_scalar(nrscale, rscale, -1.0, None, ALU.mult)
            link(8, nc.vector.tensor_scalar(sc_hi.bitcast(I32), scale.bitcast(I32), TOP12, None, ALU.bitwise_and))
            nc.vector.tensor_tensor(sc_lo, scale, sc_hi, ALU.subtract)
            link(9, nc.vector.tensor_scalar(quo[:, :], wf_raw[:, :], rscale, None, ALU.mult))
            normalise(0, 1)
            statistics(1, 0)
            link(10, nc.vector.tensor_scalar(quo_hi[:, :].bitcast(I32), quo[:, :].bitcast(I32), TOP12, None,
                                             ALU.bitwise_and))
            nc.vector.scalar_tensor_tensor(res[:, 0, :], quo_hi[:, :], sc_hi, wf_raw[:, :], ALU.mult, ALU.subtract)
            link(11, nc.vector.tensor_tensor(quo_lo[:, :], quo[:, :], quo_hi[:, :], ALU.subtract))
            link(12, nc.vector.scalar_tensor_tensor(res[:, 1, :], quo_hi[:, :], sc_lo, res[:, 0, :], ALU.mult, ALU.add))
            link(13, nc.vector.scalar_tensor_tensor(res[:, 2, :], quo_lo[:, :], sc_hi, res[:, 1, :], ALU.mult, ALU.add))
            link(14, nc.vector.scalar_tensor_tensor(res[:, 3, :], quo_lo[:, :], sc_lo, res[:, 2, :], ALU.mult, ALU.add))
            link(15, nc.vector.scalar_tensor_tensor(quo2[:, :], res[:, 3, :], nrscale, quo[:, :], ALU.mult, ALU.add))
            dve.wait_ge(consts_set, 1)
            mask_scores(0, 0)
            link(16, nc.vector.tensor_scalar(qint[:, :], quo2[:, :], ROUND, ROUND, ALU.add, ALU.subtract))
            link(17, nc.vector.tensor_scalar(qclip[:, :], qint[:, :], QMAX, -QMAX - 1.0, ALU.min, ALU.max))
            nc.vector.tensor_scalar(wq4[:, :], qclip[:, :], scale, None, ALU.mult).then_inc(wq4_ready, 1)

            def step(i, h, following, second, third):
                if second:
                    normalise(*second)
                if third:
                    statistics(*third)
                if following:
                    mask_scores(*following)
                add_residual(i, h)
                second_norm(i, h)

            dve.wait_ge(lnw_in, 16)
            with dve.Fori(0, B - 2) as i:
                step(i, 0, (i, 1), (i + 1, 0), (i + 1, 1))
                step(i, 1, (i + 1, 0), (i + 1, 1), (i + 2, 0))
            step(B - 2, 0, (B - 2, 1), (B - 1, 0), (B - 1, 1))
            step(B - 2, 1, (B - 1, 0), (B - 1, 1), None)
            step(B - 1, 0, (B - 1, 1), None, None)
            step(B - 1, 1, None, None, None)

        @block.tensor
        def _(pe):
            def used(counter, u):
                if not isinstance(u, int) or u > 0:
                    pe.wait_ge(counter, u)

            def transpose_unit(i, h):
                u = 2 * i + h
                pe.wait_ge(xt_head_ready, u + 1)
                pe.wait_ge(xt_tail_ready, u + 1)
                used(xtT_ready, u)
                for k in range(TILES):
                    last = nc.tensor.transpose(xT_ps[:, k * C:(k + 1) * C], xt[h][:, k, :], ident[:, :])
                last.then_inc(xT_done, 1)

            def project_z(i, h):
                u = 2 * i + h
                pe.wait_ge(xtT_ready, u + 1)
                used(zT_ready, u)
                nc.tensor.matmul(z_ps[:, :], g_sb[:, :], xtT[h][:, :], start=True, stop=True).then_inc(z_done, 1)

            def scores(i, h):
                u = 2 * i + h
                pe.wait_ge(zT_ready, u + 1)
                for n in range(2):
                    used(sm_ready, 2 * u - 1 + n)
                    for k in (2 * n, 2 * n + 1):
                        for a in range(2):
                            key = k * C + a * HALF
                            queries = min(HALF + SPAN, UTOK - key)
                            col = (k - 2 * n) * REACH + a * HALF
                            last = nc.tensor.matmul(s_ps[n][a * HALF:(a + 1) * HALF, col:col + queries],
                                                    xtT[h][:, key:key + HALF], zT[h][:, key:key + queries],
                                                    start=True, stop=True)
                    if n == 1 and h == 1:
                        last = nc.tensor.matmul(s_ps[1][HALF:C, REACH + C:2 * REACH], xtT[0][:, UTOK - HALF:UTOK],
                                                zT[1][:, 0:SPAN], start=True, stop=True)
                    last.then_inc(s_done, 1)

            def mix_tokens(i, h):
                u = 2 * i + h
                pe.wait_ge(sm_ready, 2 * u + 2)
                used(sxT_ready, u)
                if h:
                    pe.wait_ge(carry_ready, i + 1)
                for k in range(TILES):
                    queries = min(REACH, UTOK - k * C)
                    last = nc.tensor.matmul(sx_ps[:, k * C:k * C + queries], xt[h][:, k, :], sm[h][:, k, 0:queries],
                                            start=(k == 0), stop=(k == TILES - 1 and not h), skip_group_check=True)
                if h:
                    last = nc.tensor.matmul(sx_ps[:, 0:SPAN], xt_carry[:, :], sm[h][:, TILES - 1, C:REACH],
                                            start=False, stop=True, skip_group_check=True)
                last.then_inc(sx_done, 1)

            def attention_out(i, h):
                u = 2 * i + h
                pe.wait_ge(sxT_ready, u + 1)
                used(att_ready, u)
                for k in range(TILES):
                    last = nc.tensor.matmul(o_ps[:, k * C:(k + 1) * C], sxT[h][:, k * C:(k + 1) * C], wv_sb[:, :],
                                            start=True, stop=True)
                last.then_inc(o_done, 1)

            def ffn(i, h):
                u = 2 * i + h
                used(xy_ready, u)
                for k in range(TILES):
                    last = nc.tensor.matmul(y_ps[:, k * C:(k + 1) * C], xtT[h][:, k * C:(k + 1) * C], wf_sb[:, :],
                                            start=True, stop=True)
                last.then_inc(y_done, 1)

            pe.wait_ge(ident_set, 1)
            pe.wait_ge(wqkv_in, 16)
            for n in range(2):
                last = nc.tensor.transpose(w_ps[:, n * C:(n + 1) * C], wqkv_sb[:, n * C:(n + 1) * C], ident[:, :])
            last.then_inc(qkT_done, 1)
            pe.wait_ge(a_in, 16)
            nc.tensor.transpose(y_ps[0:RANK, 0:C], a_sb[:, :], ident[:, :]).then_inc(aT_done, 1)
            pe.wait_ge(consts_set, 1)
            pe.wait_ge(dmax_ready, 1)
            nc.tensor.matmul(sx_ps[:, 0:C], ones[:, :], dmax[:, :], start=True, stop=True).then_inc(gmax_done, 1)
            pe.wait_ge(qk_ready, 2)
            nc.tensor.matmul(z_ps[:, 0:C], wqT[:, :], wkT[:, :], start=True, stop=True).then_inc(g_done, 1)
            transpose_unit(0, 0)
            pe.wait_ge(bv_in, 16)
            nc.tensor.matmul(o_ps[:, 0:C], centre[:, :], wqkv_sb[:, 2 * C:3 * C], start=True, stop=False)
            nc.tensor.matmul(o_ps[:, 0:C], inv_rows[0:1, :], bv_row[:, :], start=False, stop=True).then_inc(wv_done, 1)
            pe.wait_ge(g_ready, 1)
            project_z(0, 0)
            pe.wait_ge(s_ps_zeroed, 1)
            scores(0, 0)

            transpose_unit(0, 1)
            pe.wait_ge(gmax_done, 1)
            pe.wait_ge(dve_chain, 2)
            mix_tokens(0, 0)
            project_z(0, 1)
            pe.wait_ge(wv_ready, 1)
            attention_out(0, 0)
            scores(0, 1)
            pe.wait_ge(wq4_ready, 1)
            pe.wait_ge(aT_ready, 1)
            pe.wait_ge(b_in, 16)
            pe.wait_ge(biasf_in, 16)
            pe.wait_ge(lnb_in, 16)
            nc.tensor.matmul(w_ps[:, 0:C], centre[:, :], wq4[:, :], start=True, stop=False)
            nc.tensor.matmul(w_ps[:, 0:C], aT_sb[:, :], b_sb[:, :], start=False, stop=False)
            nc.tensor.matmul(w_ps[:, 0:C], inv_rows[:, :], bias_rows[:, :], start=False, stop=True).then_inc(wf_done, 1)
            pe.wait_ge(wf_ready, 1)
            ffn(0, 0)

            def step(i, h, following):
                if following:
                    transpose_unit(*following)
                mix_tokens(i, h)
                if following:
                    project_z(*following)
                attention_out(i, h)
                if following:
                    scores(*following)
                ffn(i, h)

            with pe.Fori(0, B - 1) as i:
                step(i, 1, (i + 1, 0))
                step(i + 1, 0, (i + 1, 1))
            step(B - 1, 1, None)


_INS = ['L0_attn_x', 'L0_attn_W_qkv', 'L0_attn_b_qkv', 'L0_attn_ln_w', 'L0_attn_ln_b',
        'L0_ffn_kernel', 'L0_ffn_bias', 'L0_ffn_a', 'L0_ffn_b']
_OUTS = [((4, 1024, 128), 'float32')]


def kernel(**inputs):
    import numpy as _np
    import concourse.bacc as _bacc
    from concourse import mybir as _mybir
    from concourse.bass_utils import run_bass_kernel_spmd as _run

    nc = _bacc.Bacc("TRN2", target_bir_lowering=False, num_devices=1)
    arrays, args = {}, []
    for name in _INS:
        a = _np.ascontiguousarray(inputs[name])
        arrays[f"in_{name}_dram"] = a
        args.append(nc.dram_tensor(f"in_{name}_dram", a.shape, _mybir.dt.from_np(a.dtype), kind="ExternalInput").ap())
    for i, (shape, dtype) in enumerate(_OUTS):
        dt = _mybir.dt.from_np(_np.dtype(dtype))
        args.append(nc.dram_tensor(f"out_{i}_dram", shape, dt, kind="ExternalOutput").ap())
    band_block_kernel(nc, *args)
    r = _run(nc, [arrays], core_ids=[0])
    got = tuple(r.results[0][f"out_{i}_dram"] for i in range(len(_OUTS)))
    return got[0]
```

```python
import concourse.bass as bass
from concourse import mybir
from contextlib import ExitStack

F32 = mybir.dt.float32
I32 = mybir.dt.int32
ALU = mybir.AluOpType
ACT = mybir.ActivationFunctionType
AX = mybir.AxisListType


def band_block_kernel(nc, x, w_qkv, b_qkv, ln_w, ln_b, w_ffn, bias_ffn, lora_a, lora_b, out):
    C = 128
    B, T, _ = x.shape
    TILES = 4
    UTOK = TILES * C
    HALFU = TILES // 2
    HEAD = 3
    UNITS = T // UTOK
    SPAN = 32
    REACH = C + SPAN
    HALF = C // 2
    RANK = lora_a.shape[1]
    EPS = 1e-5
    SCORE_SCALE = 1.0 / float(C * SPAN) ** 0.5
    QMAX = 7.0
    ROUND = 12582912.0
    TOP12 = -4096
    WARM = (10, 0, 0)
    assert UNITS == 2 and x.shape[2] == C

    x_v = x.rearrange("b (u k p) c -> b u p k c", u=UNITS, p=C)
    out_v = out.rearrange("b (u k p) c -> b u p k c", u=UNITS, p=C)

    with ExitStack() as ctx:
        def sb(name, shape, dt=F32):
            return ctx.enter_context(nc.sbuf_tensor(name, shape, dt))

        def pb(name, shape=(128, 512)):
            return ctx.enter_context(nc.psum_tensor(name, list(shape), F32))

        def sem(name):
            return ctx.enter_context(nc.semaphore(name))

        wqkv_sb = sb("wqkv_sb", [C, 3 * C])
        bqkv_row = sb("bqkv_row", [1, 3 * C])
        bias_rows = sb("bias_rows", [2, C])
        wf_raw = sb("wf_raw", [C, C])
        a_sb = sb("a_sb", [C, RANK])
        b_sb = sb("b_sb", [RANK, C])
        lnw_b = sb("lnw_b", [C, C])
        ident = sb("ident", [C, C])
        centre = sb("centre", [C, C])
        ones = sb("ones", [C, C])
        inv_rows = sb("inv_rows", [2, C])
        mask = sb("mask", [C, REACH])
        minus_half = sb("minus_half", [C, TILES])
        eps_col = sb("eps_col", [C, TILES])
        qkvT = sb("qkvT", [C, 3 * C])
        warm_out = sb("warm_out", [C, 1])
        g_sb = sb("g_sb", [C, C])
        wv_sb = sb("wv_sb", [C, C])
        aT_sb = sb("aT_sb", [RANK, C])
        wf_sb = sb("wf_sb", [C, C])
        small = sb("small", [C, 12])
        amax, gmax, q0, e7a, e7, scale, rscale, nrscale, sc_hi, sc_lo = (small[:, n:n + 1] for n in range(10))
        dmax = sb("dmax", [C, C])
        quo = sb("quo", [C, C])
        quo_hi = sb("quo_hi", [C, C])
        quo_lo = sb("quo_lo", [C, C])
        res = sb("res", [C, 4, C])
        quo2 = sb("quo2", [C, C])
        qint = sb("qint", [C, C])
        qclip = sb("qclip", [C, C])
        wq4 = sb("wq4", [C, C])
        x_sb = sb("x_sb", [C, B * UNITS * TILES, C])
        stats = [sb(f"stats{h}", [C, TILES, 6]) for h in range(2)]
        meanvar = [sb(f"meanvar{h}", [C, TILES, 2]) for h in range(2)]
        vareps = [sb(f"vareps{h}", [C, TILES]) for h in range(2)]
        rstd = [sb(f"rstd{h}", [C, TILES]) for h in range(2)]
        mr = [sb(f"mr{h}", [C, TILES]) for h in range(2)]
        shift = [sb(f"shift{h}", [C, TILES]) for h in range(2)]
        xt = [sb(f"xt{h}", [C, TILES, C]) for h in range(2)]
        xt_carry = sb("xt_carry", [C, C])
        xtT = [sb(f"xtT{h}", [C, UTOK]) for h in range(2)]
        zT = [sb(f"zT{h}", [C, UTOK]) for h in range(2)]
        sm = [sb(f"sm{h}", [C, TILES, REACH]) for h in range(2)]
        sxT = [sb(f"sxT{h}", [C, UTOK]) for h in range(2)]
        sq_junk = sb("sq_junk", [C, TILES, C])
        ssq = [sb(f"ssq{h}", [C, TILES]) for h in range(2)]
        vareps2 = [sb(f"vareps2{h}", [C, TILES]) for h in range(2)]
        rstd2 = [sb(f"rstd2{h}", [C, TILES]) for h in range(2)]
        att = [sb(f"att{h}", [C, TILES, C]) for h in range(2)]
        xy = [sb(f"xy{h}", [C, TILES, C]) for h in range(2)]
        res_out = [sb(f"res_out{h}", [C, TILES, C]) for h in range(2)]

        w_ps = pb("w_ps")
        xT_ps = pb("xT_ps")
        z_ps = pb("z_ps")
        s_ps = [pb(f"s_ps{n}") for n in range(2)]
        sx_ps = pb("sx_ps")
        o_ps = [pb("o_ps"), w_ps]
        y_ps = pb("y_ps")

        wqkv_in, bqkv_in, biasf_in, lnb_in, wf_in, a_in, b_in, lnw_in = (
            sem(n) for n in ("wqkv_in", "bqkv_in", "biasf_in", "lnb_in", "wf_in", "a_in", "b_in", "lnw_in"))
        x_first_in = sem("x_first_in")
        x_in = [sem(f"x_in{h}") for h in range(2)]
        stored = [sem(f"stored{h}") for h in range(2)]
        ones_set = sem("ones_set")
        ident_set = sem("ident_set")
        centre_set = sem("centre_set")
        mask_set = sem("mask_set")
        pool_chain = sem("pool_chain")
        s_ps_zeroed = sem("s_ps_zeroed")
        qkvT_done = sem("qkvT_done")
        qkvT_ready = sem("qkvT_ready")
        aT_done = sem("aT_done")
        aT_ready = sem("aT_ready")
        g_done = sem("g_done")
        g_ready = sem("g_ready")
        wv_done = sem("wv_done")
        wv_ready = sem("wv_ready")
        dmax_ready = sem("dmax_ready")
        gmax_done = sem("gmax_done")
        dve_chain = sem("dve_chain")
        wq4_ready = sem("wq4_ready")
        wf_done = sem("wf_done")
        wf_ready = sem("wf_ready")
        bn_done = sem("bn_done")
        stats_ready = sem("stats_ready")
        vareps_chain = sem("vareps_chain")
        rstd_ready = sem("rstd_ready")
        shift_chain = sem("shift_chain")
        shift_ready = sem("shift_ready")
        xt_head_ready = sem("xt_head_ready")
        xt_tail_ready = sem("xt_tail_ready")
        carry_ready = sem("carry_ready")
        xT_done = sem("xT_done")
        xtT_ready = sem("xtT_ready")
        z_done = sem("z_done")
        zT_ready = sem("zT_ready")
        s_done = sem("s_done")
        sm_ready = sem("sm_ready")
        sx_done = sem("sx_done")
        sxT_ready = sem("sxT_ready")
        o_done = sem("o_done")
        ssq_ready = sem("ssq_ready")
        rstd2_chain = sem("rstd2_chain")
        rstd2_ready = sem("rstd2_ready")
        att_ready = sem("att_ready")
        y_done = sem("y_done")
        xy_ready = sem("xy_ready")
        res_ready = [sem(f"res_ready{h}") for h in range(2)]

        def unit_of_x(i, h, k, count=1):
            first = (2 * i + h) * TILES + k
            if isinstance(first, int):
                return x_sb[:, first:first + count, :]
            return x_sb[:, bass.ds(first, count), :]

        block = ctx.enter_context(nc.Block())

        @block.sync
        def _(sp):
            for h in range(UNITS):
                sp.sem_inc(stored[h], 16)
            sp.dma_start(x_sb[:, 0:HALFU, :], x_v[0, 0, :, 0:HALFU, :]).then_inc(x_first_in, 16)
            sp.dma_start(x_sb[:, HALFU:TILES, :], x_v[0, 0, :, HALFU:TILES, :]).then_inc(x_in[0], 16)
            sp.dma_start(bqkv_row[:, :], b_qkv.rearrange("(a n) -> a n", a=1)).then_inc(bqkv_in, 16)
            sp.dma_start(x_sb[:, TILES:2 * TILES, :], x_v[0, 1]).then_inc(x_in[1], 16)
            sp.dma_start(a_sb[:, :], lora_a).then_inc(a_in, 16)
            sp.wait_ge(x_in[0], 16)
            sp.dma_start(x_sb[:, 2 * TILES:3 * TILES, :], x_v[1, 0]).then_inc(x_in[0], 16)
            sp.dma_start(b_sb[:, :], lora_b).then_inc(b_in, 16)
            sp.dma_start(bias_rows[0:1, :], bias_ffn.rearrange("(a n) -> a n", a=1)).then_inc(biasf_in, 16)
            sp.dma_start(bias_rows[1:2, :], ln_b.rearrange("(a n) -> a n", a=1)).then_inc(lnb_in, 16)
            sp.wait_ge(x_in[1], 16)
            sp.dma_start(x_sb[:, 3 * TILES:4 * TILES, :], x_v[1, 1]).then_inc(x_in[1], 16)
            sp.dma_start(lnw_b[:, :], ln_w.rearrange("(a n) -> a n", a=1).to_broadcast([C, C])).then_inc(lnw_in, 16)
            with sp.Fori(2, B) as i:
                for h in range(UNITS):
                    sp.wait_ge(x_in[h], 16 * i)
                    sp.dma_start(x_sb[:, bass.ds((2 * i + h) * TILES, TILES), :], x_v[i, h]).then_inc(x_in[h], 16)
            with sp.Fori(0, B) as i:
                for h in range(UNITS):
                    sp.wait_ge(res_ready[h], i + 1)
                    sp.dma_start(out_v[i, h], res_out[h][:, :, :]).then_inc(stored[h], 16)
            for h in range(UNITS):
                sp.wait_ge(stored[h], 16 * (B + 1))

        @block.gpsimd
        def _(pool):
            nc.gpsimd.memset(ones[:, :], 1.0).then_inc(ones_set, 1)
            nc.gpsimd.memset(centre[:, :], -1.0 / C)
            nc.gpsimd.memset(inv_rows[:, :], 1.0 / C)
            nc.gpsimd.memset(ident[:, :], 0.0)
            nc.gpsimd.memset(minus_half[:, :], -0.5)
            nc.gpsimd.memset(eps_col[:, :], EPS)
            nc.gpsimd.memset(mask[:, :], 1.0).then_inc(pool_chain, 1)
            pool.wait_ge(pool_chain, 1)
            nc.gpsimd.affine_select(out=centre[:, :], in_=centre[:, :], compare_op=ALU.not_equal,
                                    fill=1.0 - 1.0 / C, base=0, pattern=[[-1, C]],
                                    channel_multiplier=1).then_inc(centre_set, 1)
            nc.gpsimd.affine_select(out=ident[:, :], in_=ident[:, :], compare_op=ALU.not_equal, fill=1.0,
                                    base=0, pattern=[[-1, C]], channel_multiplier=1).then_inc(ident_set, 1)
            nc.gpsimd.affine_select(out=mask[:, :], in_=mask[:, :], compare_op=ALU.is_ge, fill=0.0,
                                    base=0, pattern=[[1, REACH]], channel_multiplier=-1).then_inc(pool_chain, 1)
            pool.wait_ge(pool_chain, 2)
            nc.gpsimd.affine_select(out=mask[:, :], in_=mask[:, :], compare_op=ALU.is_ge, fill=0.0,
                                    base=SPAN - 1, pattern=[[-1, REACH]],
                                    channel_multiplier=1).then_inc(mask_set, 1)

            def inverse_deviation(i, h):
                u = 2 * i + h
                pool.wait_ge(stats_ready, u + 1)
                if not isinstance(u, int) or u >= 2:
                    pool.wait_ge(xt_head_ready, u - 1)
                nc.gpsimd.tensor_tensor(vareps[h][:, :], meanvar[h][:, :, 1], eps_col[:, :],
                                        ALU.add).then_inc(vareps_chain, 1)
                pool.wait_ge(vareps_chain, u + 1)
                nc.gpsimd.tensor_tensor(rstd[h][:, :], vareps[h][:, :], minus_half[:, :],
                                        ALU.pow).then_inc(rstd_ready, 1)

            def second_norm(i, h):
                u = 2 * i + h
                pool.wait_ge(ssq_ready, u + 1)
                nc.gpsimd.tensor_tensor(vareps2[h][:, :], ssq[h][:, :], eps_col[:, :],
                                        ALU.add).then_inc(rstd2_chain, 1)
                pool.wait_ge(rstd2_chain, u + 1)
                nc.gpsimd.tensor_tensor(rstd2[h][:, :], vareps2[h][:, :], minus_half[:, :],
                                        ALU.pow).then_inc(rstd2_ready, 1)

            def finish(i, h):
                u = 2 * i + h
                pool.wait_ge(att_ready, u + 1)
                pool.wait_ge(xy_ready, u + 1)
                pool.wait_ge(stored[h], 16 * (i + 1))
                nc.gpsimd.tensor_tensor(res_out[h][:, :, :], att[h][:, :, :], xy[h][:, :, :],
                                        ALU.add).then_inc(res_ready[h], 1)

            for u in range(3):
                inverse_deviation(u // 2, u % 2)
            with pool.Fori(0, B - 2) as i:
                for h in range(UNITS):
                    inverse_deviation(*((i + 1, 1), (i + 2, 0))[h])
                    second_norm(i, h)
                    finish(i, h)
            for u in range(2 * (B - 2), 2 * B):
                if u == 2 * (B - 2):
                    inverse_deviation(B - 1, 1)
                second_norm(u // 2, u % 2)
                finish(u // 2, u % 2)

        @block.scalar
        def _(act):
            act.dma_start(wqkv_sb[:, :], w_qkv).then_inc(wqkv_in, 16)
            act.dma_start(wf_raw[:, :], w_ffn).then_inc(wf_in, 16)
            act.wait_ge(ones_set, 1)
            nc.scalar.activation(warm_out[:, :], ones[:, 0:1], ACT.Square)

            def evacuate_xT(i, h):
                act.wait_ge(xT_done, 2 * i + h + 1)
                nc.scalar.activation(xtT[h][:, :], xT_ps[:, :], ACT.Copy).then_inc(xtT_ready, 1)

            def evacuate_z(i, h):
                act.wait_ge(z_done, 2 * i + h + 1)
                nc.scalar.activation(zT[h][:, :], z_ps[:, :], ACT.Copy).then_inc(zT_ready, 1)

            def evacuate_sx(i, h):
                act.wait_ge(sx_done, 2 * i + h + 1)
                nc.scalar.activation(sxT[h][:, :], sx_ps[:, :], ACT.Copy).then_inc(sxT_ready, 1)

            def square_sums(i, h):
                act.wait_ge(o_done, 2 * i + h + 1)
                for k in range(TILES):
                    last = nc.scalar.activation(sq_junk[:, k, :], o_ps[h][:, k * C:(k + 1) * C], ACT.Square,
                                                scale=float(C) ** -0.5,
                                                accum_out=ssq[h][:, k:k + 1])
                last.then_inc(ssq_ready, 1)

            def keep_carry(i):
                act.wait_ge(xt_tail_ready, 2 * i + 1)
                if not isinstance(i, int) or i > 0:
                    act.wait_ge(sx_done, 2 * i)
                nc.scalar.activation(xt_carry[:, :], xt[0][:, TILES - 1, :], ACT.Copy).then_inc(carry_ready, 1)

            def normalise(i, h, k, head=HEAD):
                if k == 0:
                    act.wait_ge(shift_ready, 2 * i + h + 1)
                ins = nc.scalar.activation(xt[h][:, k:k + 1, :], unit_of_x(i, h, k), ACT.Identity,
                                           scale=rstd[h][:, k:k + 1], bias=shift[h][:, k:k + 1])
                if k == head - 1:
                    ins.then_inc(xt_head_ready, 1)

            act.wait_ge(qkvT_done, 1)
            nc.scalar.activation(qkvT[:, :], w_ps[:, 0:3 * C], ACT.Copy).then_inc(qkvT_ready, 1)
            for k in range(HALFU):
                normalise(0, 0, k, HALFU)
            act.wait_ge(g_done, 1)
            nc.scalar.activation(g_sb[:, :], z_ps[:, 0:C], ACT.Copy, scale=SCORE_SCALE).then_inc(g_ready, 1)
            evacuate_xT(0, 0)
            act.wait_ge(aT_done, 1)
            nc.scalar.activation(aT_sb[:, :], y_ps[0:RANK, 0:C], ACT.Copy).then_inc(aT_ready, 1)
            act.wait_ge(wv_done, 1)
            nc.scalar.activation(wv_sb[:, :], o_ps[0][:, 0:C], ACT.Copy).then_inc(wv_ready, 1)
            keep_carry(0)
            evacuate_z(0, 0)

            def step(i, h, following, second):
                if following:
                    evacuate_xT(*following)
                evacuate_sx(i, h)
                if second:
                    normalise(*second, 0)
                if following:
                    evacuate_z(*following)
                if second:
                    normalise(*second, 1)
                square_sums(i, h)
                if second:
                    normalise(*second, 2)
                if h and following:
                    keep_carry(i + 1)

            for k in range(HEAD):
                normalise(0, 1, k)
            evacuate_xT(0, 1)
            evacuate_sx(0, 0)
            normalise(1, 0, 0)
            evacuate_z(0, 1)
            normalise(1, 0, 1)
            square_sums(0, 0)
            act.wait_ge(wf_done, 1)
            nc.scalar.activation(wf_sb[:, :], w_ps[:, 0:C], ACT.Copy).then_inc(wf_ready, 1)
            normalise(1, 0, 2)
            with act.Fori(0, B - 2) as i:
                step(i, 1, (i + 1, 0), (i + 1, 1))
                step(i + 1, 0, (i + 1, 1), (i + 2, 0))
            step(B - 2, 1, (B - 1, 0), (B - 1, 1))
            step(B - 1, 0, (B - 1, 1), None)
            step(B - 1, 1, None, None)

        @block.vector
        def _(dve):
            def link(count, ins):
                ins.then_inc(dve_chain, 1)
                dve.wait_ge(dve_chain, count)

            def moments(i, h):
                dve.wait_ge(x_in[h], 16 * (i + 1))
                for k in range(TILES):
                    last = nc.vector.bn_stats(stats[h][:, k, :], unit_of_x(i, h, k))
                last.then_inc(bn_done, 1)

            def aggregate(h):
                for k in range(TILES):
                    last = nc.vector.bn_aggr(meanvar[h][:, k, :], stats[h][:, k, :])
                last.then_inc(stats_ready, 1)

            def make_shift(i, h):
                u = 2 * i + h
                dve.wait_ge(rstd_ready, u + 1)
                nc.vector.scalar_tensor_tensor(mr[h][:, :], meanvar[h][:, :, 0], -1.0, rstd[h][:, :],
                                               ALU.mult, ALU.mult).then_inc(shift_chain, 1)
                dve.wait_ge(shift_chain, u + 1)
                nc.vector.tensor_scalar(shift[h][:, :], mr[h][:, :], 1.0, None, ALU.add).then_inc(shift_ready, 1)

            def normalise(i, h, head=HEAD):
                u = 2 * i + h
                if not isinstance(u, int) or u >= 2:
                    dve.wait_ge(sx_done, u - 1)
                    if h == 0:
                        dve.wait_ge(carry_ready, i)
                dve.wait_ge(shift_ready, u + 1)
                for k in range(head, TILES):
                    last = nc.vector.tensor_scalar(xt[h][:, k:k + 1, :], unit_of_x(i, h, k), rstd[h][:, k:k + 1],
                                                   shift[h][:, k:k + 1], ALU.mult, ALU.add)
                last.then_inc(xt_tail_ready, 1)

            def mask_scores(i, h, n):
                dve.wait_ge(s_done, 2 * (2 * i + h) + n + 1)
                nc.vector.tensor_tensor(
                    sm[h][:, 2 * n:2 * n + 2, :],
                    s_ps[n][:, 0:2 * REACH].rearrange("p (k r) -> p k r", k=2),
                    mask[:, :].unsqueeze(1).to_broadcast([C, 2, REACH]), ALU.mult).then_inc(sm_ready, 1)

            def add_residual(i, h):
                dve.wait_ge(y_done, 2 * i + h + 1)
                nc.vector.tensor_tensor(xy[h][:, :, :], y_ps[:, :].rearrange("p (k c) -> p k c", k=TILES),
                                        unit_of_x(i, h, 0, TILES), ALU.add).then_inc(xy_ready, 1)

            def second_norm(i, h):
                dve.wait_ge(rstd2_ready, 2 * i + h + 1)
                for k in range(TILES):
                    last = nc.vector.scalar_tensor_tensor(att[h][:, k, :], o_ps[h][:, k * C:(k + 1) * C],
                                                          rstd2[h][:, k:k + 1], lnw_b[:, :], ALU.mult, ALU.mult)
                last.then_inc(att_ready, 1)

            nc.vector.memset(s_ps[0][:, :], 0.0)
            nc.vector.memset(s_ps[1][:, :], 0.0).then_inc(s_ps_zeroed, 1)
            dve.wait_ge(x_first_in, 16)
            for k in range(TILES):
                if k == HALFU:
                    dve.wait_ge(x_in[0], 16)
                last = nc.vector.bn_stats(stats[0][:, k, :], x_sb[:, k, :])
            last.then_inc(bn_done, 1)
            dve.wait_ge(bn_done, 1)
            aggregate(0)
            dve.wait_ge(wf_in, 16)
            link(1, nc.vector.tensor_reduce(amax, wf_raw[:, :], AX.X, ALU.max, apply_absolute_value=True))
            dve.wait_ge(ident_set, 1)
            nc.vector.tensor_scalar(dmax[:, :], ident[:, :], amax, None, ALU.mult).then_inc(dmax_ready, 1)
            moments(0, 1)
            make_shift(0, 0)
            normalise(0, 0, HALFU)
            dve.wait_ge(bn_done, 2)
            aggregate(1)
            dve.wait_ge(gmax_done, 1)
            link(2, nc.vector.tensor_reduce(gmax, sx_ps[:, 0:C], AX.X, ALU.max))
            link(3, nc.vector.tensor_scalar(q0, gmax, 1.0 / QMAX, None, ALU.mult))
            link(4, nc.vector.scalar_tensor_tensor(e7a, q0, -(QMAX + 1.0), gmax, ALU.mult, ALU.add))
            link(5, nc.vector.tensor_tensor(e7, e7a, q0, ALU.add))
            link(6, nc.vector.scalar_tensor_tensor(scale, e7, 1.0 / QMAX, q0, ALU.mult, ALU.add))
            link(7, nc.vector.reciprocal(rscale, scale))
            nc.vector.tensor_scalar(nrscale, rscale, -1.0, None, ALU.mult)
            link(8, nc.vector.tensor_scalar(sc_hi.bitcast(I32), scale.bitcast(I32), TOP12, None, ALU.bitwise_and))
            nc.vector.tensor_tensor(sc_lo, scale, sc_hi, ALU.subtract)
            link(9, nc.vector.tensor_scalar(quo[:, :], wf_raw[:, :], rscale, None, ALU.mult))
            make_shift(0, 1)
            normalise(0, 1)
            moments(1, 0)
            dve.wait_ge(bn_done, 3)
            aggregate(0)
            dve.wait_ge(mask_set, 1)
            for n in range(2):
                mask_scores(0, 0, n)
            link(10, nc.vector.tensor_scalar(quo_hi[:, :].bitcast(I32), quo[:, :].bitcast(I32), TOP12, None,
                                             ALU.bitwise_and))
            nc.vector.scalar_tensor_tensor(res[:, 0, :], quo_hi[:, :], sc_hi, wf_raw[:, :], ALU.mult, ALU.subtract)
            link(11, nc.vector.tensor_tensor(quo_lo[:, :], quo[:, :], quo_hi[:, :], ALU.subtract))
            link(12, nc.vector.scalar_tensor_tensor(res[:, 1, :], quo_hi[:, :], sc_lo, res[:, 0, :], ALU.mult, ALU.add))
            link(13, nc.vector.scalar_tensor_tensor(res[:, 2, :], quo_lo[:, :], sc_hi, res[:, 1, :], ALU.mult, ALU.add))
            link(14, nc.vector.scalar_tensor_tensor(res[:, 3, :], quo_lo[:, :], sc_lo, res[:, 2, :], ALU.mult, ALU.add))
            link(15, nc.vector.scalar_tensor_tensor(quo2[:, :], res[:, 3, :], nrscale, quo[:, :], ALU.mult, ALU.add))
            make_shift(1, 0)
            link(16, nc.vector.tensor_scalar(qint[:, :], quo2[:, :], ROUND, ROUND, ALU.add, ALU.subtract))
            link(17, nc.vector.tensor_scalar(qclip[:, :], qint[:, :], QMAX, -QMAX - 1.0, ALU.min, ALU.max))
            nc.vector.tensor_scalar(wq4[:, :], qclip[:, :], scale, None, ALU.mult).then_inc(wq4_ready, 1)

            def step(i, h, following, second, third):
                if third:
                    moments(*third)
                    dve.wait_ge(bn_done, 2 * third[0] + third[1] + 1)
                if second:
                    normalise(*second)
                if third:
                    aggregate(third[1])
                if following:
                    for n in range(2):
                        mask_scores(*following, n)
                if third:
                    make_shift(*third)
                add_residual(i, h)
                second_norm(i, h)

            dve.wait_ge(lnw_in, 16)
            with dve.Fori(0, B - 2) as i:
                step(i, 0, (i, 1), (i + 1, 0), (i + 1, 1))
                step(i, 1, (i + 1, 0), (i + 1, 1), (i + 2, 0))
            step(B - 2, 0, (B - 2, 1), (B - 1, 0), (B - 1, 1))
            step(B - 2, 1, (B - 1, 0), (B - 1, 1), None)
            step(B - 1, 0, (B - 1, 1), None, None)
            step(B - 1, 1, None, None, None)

        @block.tensor
        def _(pe):
            def used(counter, u):
                if not isinstance(u, int) or u > 0:
                    pe.wait_ge(counter, u)

            def transpose_unit(i, h):
                u = 2 * i + h
                pe.wait_ge(xt_head_ready, u + 1)
                pe.wait_ge(xt_tail_ready, u + 1)
                used(xtT_ready, u)
                for k in range(TILES):
                    last = nc.tensor.transpose(xT_ps[:, k * C:(k + 1) * C], xt[h][:, k, :], ident[:, :])
                last.then_inc(xT_done, 1)

            def project_z(i, h):
                u = 2 * i + h
                pe.wait_ge(xtT_ready, u + 1)
                used(zT_ready, u)
                nc.tensor.matmul(z_ps[:, :], g_sb[:, :], xtT[h][:, :], start=True, stop=True).then_inc(z_done, 1)

            def scores(i, h):
                u = 2 * i + h
                pe.wait_ge(zT_ready, u + 1)
                for n in range(2):
                    used(sm_ready, 2 * u - 1 + n)
                    for k in (2 * n, 2 * n + 1):
                        for a in range(2):
                            key = k * C + a * HALF
                            queries = min(HALF + SPAN, UTOK - key)
                            col = (k - 2 * n) * REACH + a * HALF
                            last = nc.tensor.matmul(s_ps[n][a * HALF:(a + 1) * HALF, col:col + queries],
                                                    xtT[h][:, key:key + HALF], zT[h][:, key:key + queries],
                                                    start=True, stop=True)
                    if n == 1 and h == 1:
                        last = nc.tensor.matmul(s_ps[1][HALF:C, REACH + C:2 * REACH], xtT[0][:, UTOK - HALF:UTOK],
                                                zT[1][:, 0:SPAN], start=True, stop=True)
                    last.then_inc(s_done, 1)

            def mix_tokens(i, h):
                u = 2 * i + h
                pe.wait_ge(sm_ready, 2 * u + 2)
                used(sxT_ready, u)
                if h:
                    pe.wait_ge(carry_ready, i + 1)
                for k in range(TILES):
                    queries = min(REACH, UTOK - k * C)
                    last = nc.tensor.matmul(sx_ps[:, k * C:k * C + queries], xt[h][:, k, :], sm[h][:, k, 0:queries],
                                            start=(k == 0), stop=(k == TILES - 1 and not h), skip_group_check=True)
                if h:
                    last = nc.tensor.matmul(sx_ps[:, 0:SPAN], xt_carry[:, :], sm[h][:, TILES - 1, C:REACH],
                                            start=False, stop=True, skip_group_check=True)
                last.then_inc(sx_done, 1)

            def attention_out(i, h):
                u = 2 * i + h
                pe.wait_ge(sxT_ready, u + 1)
                used(att_ready, u - 1)
                for k in range(TILES):
                    last = nc.tensor.matmul(o_ps[h][:, k * C:(k + 1) * C], sxT[h][:, k * C:(k + 1) * C], wv_sb[:, :],
                                            start=True, stop=True)
                last.then_inc(o_done, 1)

            def ffn(i, h):
                u = 2 * i + h
                used(xy_ready, u)
                for k in range(TILES):
                    last = nc.tensor.matmul(y_ps[:, k * C:(k + 1) * C], xtT[h][:, k * C:(k + 1) * C], wf_sb[:, :],
                                            start=True, stop=True)
                last.then_inc(y_done, 1)

            def keep_busy(count, bank):
                for _ in range(count):
                    nc.tensor.matmul(bank[:, 0:C], ones[:, :], ones[:, :], start=True, stop=True)

            pe.wait_ge(ones_set, 1)
            keep_busy(WARM[0], o_ps[0])
            pe.wait_ge(centre_set, 1)
            pe.wait_ge(wqkv_in, 16)
            pe.wait_ge(bqkv_in, 16)
            for n in range(3):
                cols = slice(n * C, (n + 1) * C)
                nc.tensor.matmul(w_ps[:, cols], wqkv_sb[:, cols], centre[:, :], start=True, stop=False)
                last = nc.tensor.matmul(w_ps[:, cols], bqkv_row[:, cols], inv_rows[0:1, :], start=False, stop=True)
            last.then_inc(qkvT_done, 1)
            pe.wait_ge(dmax_ready, 1)
            nc.tensor.matmul(sx_ps[:, 0:C], ones[:, :], dmax[:, :], start=True, stop=True).then_inc(gmax_done, 1)
            pe.wait_ge(qkvT_ready, 1)
            nc.tensor.matmul(z_ps[:, 0:C], qkvT[:, 0:C], qkvT[:, C:2 * C], start=True, stop=True).then_inc(g_done, 1)
            keep_busy(WARM[1], w_ps)
            pe.wait_ge(ident_set, 1)
            transpose_unit(0, 0)
            pe.wait_ge(a_in, 16)
            nc.tensor.matmul(y_ps[0:RANK, 0:C], a_sb[:, :], centre[:, :], start=True, stop=True).then_inc(aT_done, 1)
            nc.tensor.matmul(o_ps[0][:, 0:C], qkvT[:, 2 * C:3 * C], centre[:, :], start=True, stop=True).then_inc(wv_done, 1)
            keep_busy(WARM[2], w_ps)
            pe.wait_ge(g_ready, 1)
            project_z(0, 0)
            pe.wait_ge(s_ps_zeroed, 1)
            scores(0, 0)

            transpose_unit(0, 1)
            pe.wait_ge(gmax_done, 1)
            pe.wait_ge(dve_chain, 2)
            mix_tokens(0, 0)
            project_z(0, 1)
            pe.wait_ge(wv_ready, 1)
            attention_out(0, 0)
            scores(0, 1)
            pe.wait_ge(wq4_ready, 1)
            pe.wait_ge(aT_ready, 1)
            pe.wait_ge(b_in, 16)
            pe.wait_ge(biasf_in, 16)
            pe.wait_ge(lnb_in, 16)
            nc.tensor.matmul(w_ps[:, 0:C], centre[:, :], wq4[:, :], start=True, stop=False)
            nc.tensor.matmul(w_ps[:, 0:C], aT_sb[:, :], b_sb[:, :], start=False, stop=False)
            nc.tensor.matmul(w_ps[:, 0:C], inv_rows[:, :], bias_rows[:, :], start=False, stop=True).then_inc(wf_done, 1)
            pe.wait_ge(wf_ready, 1)
            ffn(0, 0)

            def step(i, h, following):
                if following:
                    transpose_unit(*following)
                mix_tokens(i, h)
                if following:
                    project_z(*following)
                attention_out(i, h)
                if following:
                    scores(*following)
                ffn(i, h)

            step(0, 1, (1, 0))
            with pe.Fori(0, B - 2) as i:
                step(i + 1, 0, (i + 1, 1))
                step(i + 1, 1, (i + 2, 0))
            step(B - 1, 0, (B - 1, 1))
            step(B - 1, 1, None)


_INS = ['L0_attn_x', 'L0_attn_W_qkv', 'L0_attn_b_qkv', 'L0_attn_ln_w', 'L0_attn_ln_b',
        'L0_ffn_kernel', 'L0_ffn_bias', 'L0_ffn_a', 'L0_ffn_b']
_OUTS = [((4, 1024, 128), 'float32')]


def kernel(**inputs):
    import numpy as _np
    import concourse.bacc as _bacc
    from concourse import mybir as _mybir
    from concourse.bass_utils import run_bass_kernel_spmd as _run

    nc = _bacc.Bacc("TRN2", target_bir_lowering=False, num_devices=1)
    arrays, args = {}, []
    for name in _INS:
        a = _np.ascontiguousarray(inputs[name])
        arrays[f"in_{name}_dram"] = a
        args.append(nc.dram_tensor(f"in_{name}_dram", a.shape, _mybir.dt.from_np(a.dtype), kind="ExternalInput").ap())
    for i, (shape, dtype) in enumerate(_OUTS):
        dt = _mybir.dt.from_np(_np.dtype(dtype))
        args.append(nc.dram_tensor(f"out_{i}_dram", shape, dt, kind="ExternalOutput").ap())
    band_block_kernel(nc, *args)
    r = _run(nc, [arrays], core_ids=[0])
    got = tuple(r.results[0][f"out_{i}_dram"] for i in range(len(_OUTS)))
    return got[0]
```

```python
import concourse.bass as bass
from concourse import mybir
from contextlib import ExitStack

F32 = mybir.dt.float32
I32 = mybir.dt.int32
ALU = mybir.AluOpType
ACT = mybir.ActivationFunctionType
AX = mybir.AxisListType


def band_block_kernel(nc, x, w_qkv, b_qkv, ln_w, ln_b, w_ffn, bias_ffn, lora_a, lora_b, out):
    C = 128
    B, T, _ = x.shape
    TILES = 4
    UTOK = TILES * C
    HALFU = TILES // 2
    HTOK = HALFU * C
    HEAD = 2
    UNITS = T // UTOK
    SPAN = 32
    REACH = C + SPAN
    GROUPS = C // SPAN
    RANK = lora_a.shape[1]
    EPS = 1e-5
    SCORE_SCALE = 1.0 / float(C * SPAN) ** 0.5
    QMAX = 7.0
    ROUND = 12582912.0
    TOP12 = -4096
    EARLY = 1
    WARM = 9
    assert UNITS == 2 and x.shape[2] == C

    x_v = x.rearrange("b (u k p) c -> b u p k c", u=UNITS, p=C)
    out_v = out.rearrange("b (u k p) c -> b u p k c", u=UNITS, p=C)

    with ExitStack() as ctx:
        def sb(name, shape, dt=F32):
            return ctx.enter_context(nc.sbuf_tensor(name, shape, dt))

        def pb(name, shape=(128, 512)):
            return ctx.enter_context(nc.psum_tensor(name, list(shape), F32))

        def sem(name):
            return ctx.enter_context(nc.semaphore(name))

        wqkv_sb = sb("wqkv_sb", [C, 3 * C])
        bqkv_rows = sb("bqkv_rows", [3, C])
        bias_share = sb("bias_share", [C, 3])
        bias_rows = sb("bias_rows", [2, C])
        wf_raw = sb("wf_raw", [C, C])
        a_sb = sb("a_sb", [C, RANK])
        b_sb = sb("b_sb", [RANK, C])
        lnw_b = sb("lnw_b", [C, C])
        ident = sb("ident", [C, C])
        centre = sb("centre", [C, C])
        ones = sb("ones", [C, C])
        inv_rows = sb("inv_rows", [2, C])
        mask = sb("mask", [C, REACH])
        minus_half = sb("minus_half", [C, TILES])
        eps_col = sb("eps_col", [C, TILES])
        qkvT = sb("qkvT", [C, 3 * C])
        warm_out = sb("warm_out", [C, 1])
        g_sb = sb("g_sb", [C, C])
        wv_sb = sb("wv_sb", [C, C])
        aT_sb = sb("aT_sb", [RANK, C])
        wf_sb = sb("wf_sb", [C, C])
        small = sb("small", [C, 12])
        amax, gmax, q0, e7a, e7, scale, rscale, nrscale, sc_hi, sc_lo = (small[:, n:n + 1] for n in range(10))
        dmax = sb("dmax", [C, C])
        quo = sb("quo", [C, C])
        quo_hi = sb("quo_hi", [C, C])
        quo_lo = sb("quo_lo", [C, C])
        res = sb("res", [C, 4, C])
        quo2 = sb("quo2", [C, C])
        qint = sb("qint", [C, C])
        qclip = sb("qclip", [C, C])
        wq4 = sb("wq4", [C, C])
        x_sb = sb("x_sb", [C, B * UNITS * TILES, C])
        stats = [sb(f"stats{h}", [C, TILES, 6]) for h in range(2)]
        meanvar = [sb(f"meanvar{h}", [C, TILES, 2]) for h in range(2)]
        vareps = [sb(f"vareps{h}", [C, TILES]) for h in range(2)]
        rstd = [sb(f"rstd{h}", [C, TILES]) for h in range(2)]
        mr = [sb(f"mr{h}", [C, TILES]) for h in range(2)]
        shift = [sb(f"shift{h}", [C, TILES]) for h in range(2)]
        xt = [sb(f"xt{h}", [C, TILES, C]) for h in range(2)]
        xt_carry = sb("xt_carry", [C, C])
        xtT = [sb(f"xtT{h}", [C, UTOK]) for h in range(2)]
        zT = [sb(f"zT{h}", [C, UTOK]) for h in range(2)]
        sm = [sb(f"sm{h}", [C, TILES, REACH]) for h in range(2)]
        sxT = [sb(f"sxT{h}", [C, UTOK]) for h in range(2)]
        sq_junk = sb("sq_junk", [C, TILES, C])
        ssq = [sb(f"ssq{h}", [C, TILES]) for h in range(2)]
        vareps2 = [sb(f"vareps2{h}", [C, TILES]) for h in range(2)]
        rstd2 = [sb(f"rstd2{h}", [C, TILES]) for h in range(2)]
        att = [sb(f"att{h}", [C, TILES, C]) for h in range(2)]
        xy = [sb(f"xy{h}", [C, TILES, C]) for h in range(2)]
        res_out = [sb(f"res_out{h}", [C, TILES, C]) for h in range(2)]

        w_ps = pb("w_ps")
        xT_ps = pb("xT_ps")
        z_ps = pb("z_ps")
        s_ps = [pb(f"s_ps{n}") for n in range(2)]
        sx_ps = pb("sx_ps")
        o_ps = [pb("o_ps"), w_ps]
        y_ps = pb("y_ps")
        qkvT_ps = (w_ps, xT_ps, y_ps)
        first_xT = (xT_ps, w_ps)
        first_z = (z_ps, sx_ps)
        last_sx = (sx_ps, z_ps)
        last_o = (w_ps, xT_ps)
        last_y = (y_ps, s_ps[0])

        wqkv_in, bqkv_in, biasf_in, lnb_in, wf_in, a_in, b_in, lnw_in = (
            sem(n) for n in ("wqkv_in", "bqkv_in", "biasf_in", "lnb_in", "wf_in", "a_in", "b_in", "lnw_in"))
        x_first_in = sem("x_first_in")
        x_in = [sem(f"x_in{h}") for h in range(2)]
        stored = [sem(f"stored{h}") for h in range(2)]
        ones_set = sem("ones_set")
        ident_set = sem("ident_set")
        centre_set = sem("centre_set")
        mask_set = sem("mask_set")
        pool_chain = sem("pool_chain")
        s_ps_zeroed = sem("s_ps_zeroed")
        bias_done = sem("bias_done")
        bias_share_chain = sem("bias_share_chain")
        qkvT_done = sem("qkvT_done")
        qkvT_ready = sem("qkvT_ready")
        aT_done = sem("aT_done")
        aT_ready = sem("aT_ready")
        g_done = sem("g_done")
        g_ready = sem("g_ready")
        wv_done = sem("wv_done")
        wv_ready = sem("wv_ready")
        dmax_ready = sem("dmax_ready")
        gmax_done = sem("gmax_done")
        dve_chain = sem("dve_chain")
        wq4_ready = sem("wq4_ready")
        wf_done = sem("wf_done")
        wf_ready = sem("wf_ready")
        bn_done = sem("bn_done")
        stats_ready = sem("stats_ready")
        vareps_chain = sem("vareps_chain")
        rstd_ready = sem("rstd_ready")
        shift_chain = sem("shift_chain")
        shift_ready = sem("shift_ready")
        xt_head_ready = sem("xt_head_ready")
        xt_tail_ready = sem("xt_tail_ready")
        carry_ready = sem("carry_ready")
        xT_done = sem("xT_done")
        xtT_ready = sem("xtT_ready")
        z_done = sem("z_done")
        zT_ready = sem("zT_ready")
        s_done = sem("s_done")
        sm_ready = sem("sm_ready")
        sx_done = sem("sx_done")
        sxT_ready = sem("sxT_ready")
        o_done = sem("o_done")
        ssq_ready = sem("ssq_ready")
        rstd2_chain = sem("rstd2_chain")
        rstd2_ready = sem("rstd2_ready")
        att_ready = sem("att_ready")
        y_done = sem("y_done")
        xy_ready = sem("xy_ready")
        res_ready = [sem(f"res_ready{h}") for h in range(2)]
        half_xT_done = (sem("first_xT_done"), xT_done)
        half_xtT_ready = (sem("first_xtT_ready"), xtT_ready)
        half_z_done = (sem("first_z_done"), z_done)
        half_zT_ready = (sem("first_zT_ready"), zT_ready)
        half_sx_done = sem("half_sx_done")
        half_sxT_ready = sem("half_sxT_ready")
        half_o_done = sem("half_o_done")
        half_y_done = sem("half_y_done")
        half_ssq_ready = sem("half_ssq_ready")
        half_vareps2_ready = sem("half_vareps2_ready")
        weighted = sem("weighted")

        def unit_of_x(i, h, k, count=1):
            first = (2 * i + h) * TILES + k
            if isinstance(first, int):
                return x_sb[:, first:first + count, :]
            return x_sb[:, bass.ds(first, count), :]

        block = ctx.enter_context(nc.Block())

        @block.sync
        def _(sp):
            sp.dma_start(x_sb[:, HALFU:TILES, :], x_v[0, 0, :, HALFU:TILES, :]).then_inc(x_in[0], 16)
            sp.dma_start(x_sb[:, TILES:2 * TILES, :], x_v[0, 1]).then_inc(x_in[1], 16)
            sp.dma_start(wf_raw[:, :], w_ffn).then_inc(wf_in, 16)
            for h in range(UNITS):
                sp.sem_inc(stored[h], 16)
            sp.wait_ge(x_in[0], 16)
            sp.dma_start(x_sb[:, 2 * TILES:3 * TILES, :], x_v[1, 0]).then_inc(x_in[0], 16)
            sp.dma_start(a_sb[:, :], lora_a).then_inc(a_in, 16)
            sp.dma_start(b_sb[:, :], lora_b).then_inc(b_in, 16)
            sp.dma_start(bias_rows[0:1, :], bias_ffn.rearrange("(a n) -> a n", a=1)).then_inc(biasf_in, 16)
            sp.dma_start(bias_rows[1:2, :], ln_b.rearrange("(a n) -> a n", a=1)).then_inc(lnb_in, 16)
            sp.wait_ge(x_in[1], 16)
            sp.dma_start(x_sb[:, 3 * TILES:4 * TILES, :], x_v[1, 1]).then_inc(x_in[1], 16)
            sp.dma_start(lnw_b[:, :], ln_w.rearrange("(a n) -> a n", a=1).to_broadcast([C, C])).then_inc(lnw_in, 16)
            with sp.Fori(2, B) as i:
                for h in range(UNITS):
                    sp.wait_ge(x_in[h], 16 * i)
                    sp.dma_start(x_sb[:, bass.ds((2 * i + h) * TILES, TILES), :], x_v[i, h]).then_inc(x_in[h], 16)
            with sp.Fori(0, B - 1) as i:
                for h in range(UNITS):
                    sp.wait_ge(res_ready[h], i + 1)
                    sp.dma_start(out_v[i, h], res_out[h][:, :, :]).then_inc(stored[h], 16)
            sp.wait_ge(res_ready[0], B)
            sp.dma_start(out_v[B - 1, 0], res_out[0][:, :, :]).then_inc(stored[0], 16)
            for n in range(2):
                half = slice(n * HALFU, (n + 1) * HALFU)
                sp.wait_ge(res_ready[1], B + n)
                sp.dma_start(out_v[B - 1, 1, :, half, :], res_out[1][:, half, :]).then_inc(stored[1], 16)
            sp.wait_ge(stored[0], 16 * (B + 1))
            sp.wait_ge(stored[1], 16 * (B + 2))

        @block.gpsimd
        def _(pool):
            nc.gpsimd.memset(ones[:, :], 1.0).then_inc(ones_set, 1)
            nc.gpsimd.memset(centre[:, :], -1.0 / C)
            nc.gpsimd.memset(inv_rows[:, :], 1.0 / C)
            nc.gpsimd.memset(ident[:, :], 0.0)
            nc.gpsimd.memset(minus_half[:, :], -0.5)
            nc.gpsimd.memset(eps_col[:, :], EPS)
            nc.gpsimd.memset(mask[:, :], 1.0).then_inc(pool_chain, 1)
            pool.wait_ge(pool_chain, 1)
            nc.gpsimd.affine_select(out=centre[:, :], in_=centre[:, :], compare_op=ALU.not_equal,
                                    fill=1.0 - 1.0 / C, base=0, pattern=[[-1, C]],
                                    channel_multiplier=1).then_inc(centre_set, 1)
            nc.gpsimd.affine_select(out=ident[:, :], in_=ident[:, :], compare_op=ALU.not_equal, fill=1.0,
                                    base=0, pattern=[[-1, C]], channel_multiplier=1).then_inc(ident_set, 1)
            nc.gpsimd.affine_select(out=mask[:, :], in_=mask[:, :], compare_op=ALU.is_ge, fill=0.0,
                                    base=0, pattern=[[1, REACH]], channel_multiplier=-1).then_inc(pool_chain, 1)
            pool.wait_ge(pool_chain, 2)
            nc.gpsimd.affine_select(out=mask[:, :], in_=mask[:, :], compare_op=ALU.is_ge, fill=0.0,
                                    base=SPAN - 1, pattern=[[-1, REACH]],
                                    channel_multiplier=1).then_inc(mask_set, 1)

            def inverse_deviation(i, h):
                u = 2 * i + h
                pool.wait_ge(stats_ready, u + 1)
                if not isinstance(u, int) or u >= 2:
                    pool.wait_ge(xt_head_ready, u - 1)
                nc.gpsimd.tensor_tensor(vareps[h][:, :], meanvar[h][:, :, 1], eps_col[:, :],
                                        ALU.add).then_inc(vareps_chain, 1)
                pool.wait_ge(vareps_chain, u + 1)
                nc.gpsimd.tensor_tensor(rstd[h][:, :], vareps[h][:, :], minus_half[:, :],
                                        ALU.pow).then_inc(rstd_ready, 1)
                if isinstance(u, int) and u == 0:
                    return
                pool.wait_ge(rstd_ready, u + 1)
                nc.gpsimd.tensor_tensor(mr[h][:, :], meanvar[h][:, :, 0], rstd[h][:, :],
                                        ALU.mult).then_inc(shift_chain, 1)
                pool.wait_ge(shift_chain, u + 1)
                nc.gpsimd.tensor_tensor(shift[h][:, :], ones[:, 0:TILES], mr[h][:, :],
                                        ALU.subtract).then_inc(shift_ready, 1)

            def second_norm(i, h):
                u = 2 * i + h
                pool.wait_ge(ssq_ready, u + 1)
                nc.gpsimd.tensor_tensor(vareps2[h][:, :], ssq[h][:, :], eps_col[:, :],
                                        ALU.add).then_inc(rstd2_chain, 1)
                pool.wait_ge(rstd2_chain, u + 1)
                nc.gpsimd.tensor_tensor(rstd2[h][:, :], vareps2[h][:, :], minus_half[:, :],
                                        ALU.pow).then_inc(rstd2_ready, 1)

            def finish(i, h):
                u = 2 * i + h
                pool.wait_ge(att_ready, u + 1)
                pool.wait_ge(xy_ready, u + 1)
                pool.wait_ge(stored[h], 16 * (i + 1))
                nc.gpsimd.tensor_tensor(res_out[h][:, :, :], att[h][:, :, :], xy[h][:, :, :],
                                        ALU.add).then_inc(res_ready[h], 1)

            for u in range(3):
                inverse_deviation(u // 2, u % 2)
            pool.wait_ge(sx_done, 1)
            pool.wait_ge(carry_ready, 1)
            pool.wait_ge(shift_ready, 3)
            pool.wait_ge(xt_tail_ready, 2)
            for k in range(HEAD, TILES):
                last = nc.gpsimd.tensor_scalar(xt[0][:, k:k + 1, :], unit_of_x(1, 0, k), rstd[0][:, k:k + 1],
                                               shift[0][:, k:k + 1], ALU.mult, ALU.add)
            last.then_inc(xt_tail_ready, 1)
            inverse_deviation(1, 1)
            second_norm(0, 0)
            with pool.Fori(0, B - 2) as i:
                inverse_deviation(i + 2, 0)
                finish(i, 0)
                second_norm(i, 1)
                inverse_deviation(i + 2, 1)
                finish(i, 1)
                second_norm(i + 1, 0)
            finish(B - 2, 0)
            second_norm(B - 2, 1)
            finish(B - 2, 1)
            second_norm(B - 1, 0)
            for n in range(2):
                half = slice(n * HALFU, (n + 1) * HALFU)
                pool.wait_ge(half_vareps2_ready, n + 1)
                nc.gpsimd.tensor_tensor(rstd2[1][:, half], vareps2[1][:, half], minus_half[:, half],
                                        ALU.pow).then_inc(rstd2_ready, 1)

        @block.scalar
        def _(act):
            act.dma_start(x_sb[:, 0:HALFU, :], x_v[0, 0, :, 0:HALFU, :]).then_inc(x_first_in, 16)
            act.dma_start(wqkv_sb[:, :], w_qkv).then_inc(wqkv_in, 16)
            act.dma_start(bqkv_rows[:, :], b_qkv.rearrange("(n c) -> n c", c=C)).then_inc(bqkv_in, 16)
            act.wait_ge(ones_set, 1)
            nc.scalar.activation(warm_out[:, :], ones[:, 0:1], ACT.Square)

            def evacuate_xT(i, h):
                act.wait_ge(xT_done, 2 * i + h + 1)
                nc.scalar.activation(xtT[h][:, :], xT_ps[:, :], ACT.Copy).then_inc(xtT_ready, 1)

            def evacuate_z(i, h):
                act.wait_ge(z_done, 2 * i + h + 1)
                nc.scalar.activation(zT[h][:, :], z_ps[:, :], ACT.Copy).then_inc(zT_ready, 1)

            def evacuate_sx(i, h):
                act.wait_ge(sx_done, 2 * i + h + 1)
                nc.scalar.activation(sxT[h][:, :], sx_ps[:, :], ACT.Copy).then_inc(sxT_ready, 1)

            def square_sums(i, h):
                act.wait_ge(o_done, 2 * i + h + 1)
                for k in range(TILES):
                    last = nc.scalar.activation(sq_junk[:, k, :], o_ps[h][:, k * C:(k + 1) * C], ACT.Square,
                                                scale=float(C) ** -0.5,
                                                accum_out=ssq[h][:, k:k + 1])
                last.then_inc(ssq_ready, 1)

            def keep_carry(i):
                act.wait_ge(xt_tail_ready, 2 * i + 1)
                if not isinstance(i, int) or i > 0:
                    act.wait_ge(sx_done, 2 * i)
                nc.scalar.activation(xt_carry[:, :], xt[0][:, TILES - 1, :], ACT.Copy).then_inc(carry_ready, 1)

            def normalise(i, h, k, head=HEAD):
                if k == 0:
                    act.wait_ge(shift_ready, 2 * i + h + 1)
                ins = nc.scalar.activation(xt[h][:, k:k + 1, :], unit_of_x(i, h, k), ACT.Identity,
                                           scale=rstd[h][:, k:k + 1], bias=shift[h][:, k:k + 1])
                if k == head - 1:
                    ins.then_inc(xt_head_ready, 1)

            act.wait_ge(bias_done, 1)
            nc.scalar.activation(bias_share[:, :], z_ps[:, 0:3], ACT.Copy,
                                 scale=1.0 / C).then_inc(bias_share_chain, 1)
            act.wait_ge(bias_share_chain, 1)

            def evacuate_weights(n):
                act.wait_ge(qkvT_done, n + 1)
                nc.scalar.activation(qkvT[:, n * C:(n + 1) * C], qkvT_ps[n][:, 0:C], ACT.Identity,
                                     bias=bias_share[:, n:n + 1]).then_inc(qkvT_ready, 1)

            evacuate_weights(0)
            evacuate_weights(1)
            for k in range(HALFU):
                normalise(0, 0, k, HALFU)
            evacuate_weights(2)
            act.wait_ge(g_done, 1)
            nc.scalar.activation(g_sb[:, :], z_ps[:, 0:C], ACT.Copy, scale=SCORE_SCALE).then_inc(g_ready, 1)
            for n in range(2):
                act.wait_ge(half_xT_done[n], 1)
                nc.scalar.activation(xtT[0][:, n * HTOK:(n + 1) * HTOK], first_xT[n][:, 0:HTOK],
                                     ACT.Copy).then_inc(half_xtT_ready[n], 1)
            for k in range(HEAD):
                normalise(0, 1, k)
            for n in range(2):
                act.wait_ge(half_z_done[n], 1)
                nc.scalar.activation(zT[0][:, n * HTOK:(n + 1) * HTOK], first_z[n][:, 0:HTOK],
                                     ACT.Copy).then_inc(half_zT_ready[n], 1)
            evacuate_xT(0, 1)
            act.wait_ge(wv_done, 1)
            nc.scalar.activation(wv_sb[:, :], o_ps[0][:, 0:C], ACT.Copy).then_inc(wv_ready, 1)
            act.wait_ge(aT_done, 1)
            nc.scalar.activation(aT_sb[:, :], y_ps[0:RANK, 0:C], ACT.Copy).then_inc(aT_ready, 1)
            keep_carry(0)

            def step(i, h, following, second, transposed=False):
                if following and not transposed:
                    evacuate_xT(*following)
                evacuate_sx(i, h)
                if second:
                    normalise(*second, 0)
                if following:
                    evacuate_z(*following)
                if second:
                    normalise(*second, 1)
                square_sums(i, h)
                if h and following:
                    keep_carry(i + 1)

            evacuate_z(0, 1)
            evacuate_sx(0, 0)
            for k in range(HEAD):
                normalise(1, 0, k)
            act.wait_ge(wf_done, 1)
            nc.scalar.activation(wf_sb[:, :], w_ps[:, 0:C], ACT.Copy).then_inc(wf_ready, 1)
            square_sums(0, 0)
            act.wait_ge(y_done, 1)
            evacuate_xT(1, 0)
            step(0, 1, (1, 0), (1, 1), transposed=True)
            with act.Fori(1, B - 1) as i:
                step(i, 0, (i, 1), (i + 1, 0))
                step(i, 1, (i + 1, 0), (i + 1, 1))
            step(B - 1, 0, (B - 1, 1), None)
            for n in range(2):
                act.wait_ge(half_sx_done, n + 1)
                nc.scalar.activation(sxT[1][:, n * HTOK:(n + 1) * HTOK], last_sx[n][:, 0:HTOK],
                                     ACT.Copy).then_inc(half_sxT_ready, 1)
            for n in range(2):
                act.wait_ge(half_o_done, n + 1)
                for k in range(HALFU):
                    col = n * HALFU + k
                    last = nc.scalar.activation(sq_junk[:, col, :], last_o[n][:, k * C:(k + 1) * C], ACT.Square,
                                                scale=float(C) ** -0.5, accum_out=ssq[1][:, col:col + 1])
                last.then_inc(half_ssq_ready, 1)

        @block.vector
        def _(dve):
            def moments(i, h, tiles=range(TILES)):
                if tiles[0] == 0:
                    dve.wait_ge(x_in[h], 16 * (i + 1))
                for k in tiles:
                    last = nc.vector.bn_stats(stats[h][:, k, :], unit_of_x(i, h, k))
                if k == TILES - 1:
                    last.then_inc(bn_done, 1)

            def aggregate(h, tiles=range(TILES)):
                for k in tiles:
                    last = nc.vector.bn_aggr(meanvar[h][:, k, :], stats[h][:, k, :])
                if k == TILES - 1:
                    last.then_inc(stats_ready, 1)

            def normalise(i, h, head=HEAD, aggregated=None):
                u = 2 * i + h
                if not isinstance(u, int) or u >= 2:
                    dve.wait_ge(sx_done, u - 1)
                    if h == 0:
                        dve.wait_ge(carry_ready, i)
                dve.wait_ge(shift_ready, u + 1)
                for k in range(head, TILES):
                    if k == TILES - 1 and aggregated:
                        dve.wait_ge(bn_done, 2 * aggregated[0] + aggregated[1] + 1)
                    last = nc.vector.tensor_scalar(xt[h][:, k:k + 1, :], unit_of_x(i, h, k), rstd[h][:, k:k + 1],
                                                   shift[h][:, k:k + 1], ALU.mult, ALU.add)
                last.then_inc(xt_tail_ready, 1)

            def mask_scores(i, h, n):
                dve.wait_ge(s_done, 2 * (2 * i + h) + n + 1)
                nc.vector.tensor_tensor(
                    sm[h][:, 2 * n:2 * n + 2, :],
                    s_ps[n][:, 0:2 * REACH].rearrange("p (k r) -> p k r", k=2),
                    mask[:, :].unsqueeze(1).to_broadcast([C, 2, REACH]), ALU.mult).then_inc(sm_ready, 1)

            def add_residual(i, h):
                dve.wait_ge(y_done, 2 * i + h + 1)
                nc.vector.tensor_tensor(xy[h][:, :, :], y_ps[:, :].rearrange("p (k c) -> p k c", k=TILES),
                                        unit_of_x(i, h, 0, TILES), ALU.add).then_inc(xy_ready, 1)

            def second_norm(i, h):
                dve.wait_ge(rstd2_ready, 2 * i + h + 1)
                for k in range(TILES):
                    last = nc.vector.scalar_tensor_tensor(att[h][:, k, :], o_ps[h][:, k * C:(k + 1) * C],
                                                          rstd2[h][:, k:k + 1], lnw_b[:, :], ALU.mult, ALU.mult)
                last.then_inc(att_ready, 1)

            def weight(h, n, tiles, bank):
                nc.vector.tensor_tensor(att[h][:, n:n + tiles, :],
                                        bank[:, 0:tiles * C].rearrange("p (k c) -> p k c", k=tiles),
                                        lnw_b[:, :].unsqueeze(1).to_broadcast([C, tiles, C]),
                                        ALU.mult).then_inc(weighted, 1)

            def finish(h, n, tiles, sums, count):
                dve.wait_ge(rstd2_ready, count)
                for k in range(tiles):
                    last = nc.vector.scalar_tensor_tensor(res_out[h][:, n + k, :], att[h][:, n + k, :],
                                                          rstd2[h][:, n + k:n + k + 1], sums[:, k, :],
                                                          ALU.mult, ALU.add)
                last.then_inc(res_ready[h], 1)

            nc.vector.memset(s_ps[0][:, :], 0.0)
            nc.vector.memset(s_ps[1][:, :], 0.0).then_inc(s_ps_zeroed, 1)
            dve.wait_ge(x_first_in, 16)
            for k in range(TILES):
                if k == HALFU:
                    dve.wait_ge(x_in[0], 16)
                last = nc.vector.bn_stats(stats[0][:, k, :], x_sb[:, k, :])
            last.then_inc(bn_done, 1)
            dve.wait_ge(bn_done, 1)
            aggregate(0)
            moments(0, 1, range(HALFU))
            dve.wait_ge(wf_in, 16)
            nc.vector.tensor_reduce(amax, wf_raw[:, :], AX.X, ALU.max, apply_absolute_value=True).then_inc(dve_chain, 1)
            moments(0, 1, range(HALFU, TILES))
            dve.wait_ge(dve_chain, 1)
            dve.wait_ge(ident_set, 1)
            nc.vector.tensor_scalar(dmax[:, :], ident[:, :], amax, None, ALU.mult).then_inc(dmax_ready, 1)
            dve.wait_ge(bn_done, 2)
            dve.wait_ge(rstd_ready, 1)
            nc.vector.scalar_tensor_tensor(mr[0][:, :], meanvar[0][:, :, 0], -1.0, rstd[0][:, :],
                                           ALU.mult, ALU.mult).then_inc(shift_chain, 1)
            aggregate(1, range(HALFU))
            dve.wait_ge(shift_chain, 1)
            nc.vector.tensor_scalar(shift[0][:, :], mr[0][:, :], 1.0, None, ALU.add).then_inc(shift_ready, 1)
            aggregate(1, range(HALFU, TILES))
            normalise(0, 0, HALFU)
            dve.wait_ge(gmax_done, 1)
            nc.vector.tensor_reduce(gmax, sx_ps[:, 0:C], AX.X, ALU.max).then_inc(dve_chain, 1)
            dve.wait_ge(dve_chain, 2)
            nc.vector.tensor_scalar(q0, gmax, 1.0 / QMAX, None, ALU.mult).then_inc(dve_chain, 1)
            moments(1, 0, range(0, 1))
            dve.wait_ge(dve_chain, 3)
            nc.vector.scalar_tensor_tensor(e7a, q0, -(QMAX + 1.0), gmax, ALU.mult, ALU.add).then_inc(dve_chain, 1)
            moments(1, 0, range(1, 2))
            dve.wait_ge(dve_chain, 4)
            nc.vector.tensor_tensor(e7, e7a, q0, ALU.add).then_inc(dve_chain, 1)
            moments(1, 0, range(2, 3))
            dve.wait_ge(dve_chain, 5)
            nc.vector.scalar_tensor_tensor(scale, e7, 1.0 / QMAX, q0, ALU.mult, ALU.add).then_inc(dve_chain, 1)
            moments(1, 0, range(3, 4))
            dve.wait_ge(dve_chain, 6)
            dve.wait_ge(bn_done, 3)
            nc.vector.reciprocal(rscale, scale).then_inc(dve_chain, 1)
            normalise(0, 1)
            dve.wait_ge(dve_chain, 7)
            nc.vector.tensor_scalar(nrscale, rscale, -1.0, None, ALU.mult)
            nc.vector.tensor_scalar(sc_hi.bitcast(I32), scale.bitcast(I32),
                                    TOP12, None, ALU.bitwise_and).then_inc(dve_chain, 1)
            aggregate(0)
            dve.wait_ge(dve_chain, 8)
            nc.vector.tensor_tensor(sc_lo, scale, sc_hi, ALU.subtract)
            nc.vector.tensor_scalar(quo[:, :], wf_raw[:, :], rscale, None, ALU.mult).then_inc(dve_chain, 1)
            dve.wait_ge(dve_chain, 9)
            nc.vector.tensor_scalar(quo_hi[:, :].bitcast(I32), quo[:, :].bitcast(I32), TOP12, None,
                                        ALU.bitwise_and).then_inc(dve_chain, 1)
            dve.wait_ge(dve_chain, 10)
            nc.vector.scalar_tensor_tensor(res[:, 0, :], quo_hi[:, :], sc_hi, wf_raw[:, :], ALU.mult, ALU.subtract)
            nc.vector.tensor_tensor(quo_lo[:, :], quo[:, :], quo_hi[:, :], ALU.subtract).then_inc(dve_chain, 1)
            dve.wait_ge(dve_chain, 11)
            dve.wait_ge(mask_set, 1)
            mask_scores(0, 0, 0)
            mask_scores(0, 0, 1)
            nc.vector.scalar_tensor_tensor(res[:, 1, :], quo_hi[:, :], sc_lo, res[:, 0, :],
                                           ALU.mult, ALU.add).then_inc(dve_chain, 1)
            dve.wait_ge(dve_chain, 12)
            nc.vector.scalar_tensor_tensor(res[:, 2, :], quo_lo[:, :], sc_hi, res[:, 1, :],
                                           ALU.mult, ALU.add).then_inc(dve_chain, 1)
            dve.wait_ge(dve_chain, 13)
            nc.vector.scalar_tensor_tensor(res[:, 3, :], quo_lo[:, :], sc_lo, res[:, 2, :],
                                           ALU.mult, ALU.add).then_inc(dve_chain, 1)
            dve.wait_ge(dve_chain, 14)
            nc.vector.scalar_tensor_tensor(quo2[:, :], res[:, 3, :], nrscale, quo[:, :],
                                           ALU.mult, ALU.add).then_inc(dve_chain, 1)
            dve.wait_ge(dve_chain, 15)
            nc.vector.tensor_scalar(qint[:, :], quo2[:, :], ROUND, ROUND, ALU.add, ALU.subtract).then_inc(dve_chain, 1)
            moments(1, 1, range(0, 1))
            dve.wait_ge(dve_chain, 16)
            nc.vector.tensor_scalar(qclip[:, :], qint[:, :], QMAX, -QMAX - 1.0, ALU.min, ALU.max).then_inc(dve_chain, 1)
            moments(1, 1, range(1, 2))
            dve.wait_ge(dve_chain, 17)
            nc.vector.tensor_scalar(wq4[:, :], qclip[:, :], scale, None, ALU.mult).then_inc(wq4_ready, 1)

            def step(i, h, before, following, second, third):
                if third:
                    moments(*third)
                if second:
                    normalise(*second, aggregated=third)
                if third:
                    aggregate(third[1])
                if before:
                    second_norm(*before)
                for n in range(2):
                    mask_scores(*following, n)
                add_residual(i, h)

            dve.wait_ge(lnw_in, 16)
            mask_scores(0, 1, 0)
            moments(1, 1, range(2, TILES))
            mask_scores(0, 1, 1)
            dve.wait_ge(bn_done, 4)
            aggregate(1)
            add_residual(0, 0)
            with dve.Fori(0, B - 2) as i:
                step(i, 1, (i, 0), (i + 1, 0), (i + 1, 1), (i + 2, 0))
                step(i + 1, 0, (i, 1), (i + 1, 1), (i + 2, 0), (i + 2, 1))
            step(B - 2, 1, (B - 2, 0), (B - 1, 0), (B - 1, 1), None)
            second_norm(B - 2, 1)
            for n in range(2):
                mask_scores(B - 1, 1, n)
            dve.wait_ge(ssq_ready, 2 * B - 1)
            weight(0, 0, TILES, o_ps[0])
            add_residual(B - 1, 0)
            dve.wait_ge(weighted, 1)
            dve.wait_ge(xy_ready, 2 * B - 1)
            dve.wait_ge(stored[0], 16 * B)
            finish(0, 0, TILES, xy[0], 2 * B - 1)
            for n in range(2):
                half = slice(n * HALFU, (n + 1) * HALFU)
                dve.wait_ge(half_ssq_ready, n + 1)
                nc.vector.tensor_scalar(vareps2[1][:, half], ssq[1][:, half], EPS, None,
                                        ALU.add).then_inc(half_vareps2_ready, 1)
                weight(1, n * HALFU, HALFU, last_o[n])
            dve.wait_ge(weighted, 3)
            dve.wait_ge(stored[1], 16 * B)
            for n in range(2):
                dve.wait_ge(half_y_done, n + 1)
                finish(1, n * HALFU, HALFU, last_y[n][:, 0:HTOK].rearrange("p (k c) -> p k c", k=HALFU), 2 * B + n)

        @block.tensor
        def _(pe):
            def used(counter, u):
                if not isinstance(u, int) or u > 0:
                    pe.wait_ge(counter, u)

            def transpose_unit(i, h):
                u = 2 * i + h
                pe.wait_ge(xt_head_ready, u + 1)
                pe.wait_ge(xt_tail_ready, u + 1)
                used(xtT_ready, u)
                for k in range(TILES):
                    last = nc.tensor.transpose(xT_ps[:, k * C:(k + 1) * C], xt[h][:, k, :], ident[:, :])
                last.then_inc(xT_done, 1)

            def project_z(i, h):
                u = 2 * i + h
                pe.wait_ge(xtT_ready, u + 1)
                used(zT_ready, u)
                nc.tensor.matmul(z_ps[:, :], g_sb[:, :], xtT[h][:, :], start=True, stop=True).then_inc(z_done, 1)

            def scores(i, h):
                u = 2 * i + h
                pe.wait_ge(zT_ready, u + 1)
                for n in range(2):
                    used(sm_ready, 2 * u - 1 + n)
                    for k in (2 * n, 2 * n + 1):
                        for a in range(GROUPS):
                            key = k * C + a * SPAN
                            queries = min(2 * SPAN, UTOK - key)
                            col = (k - 2 * n) * REACH + a * SPAN
                            last = nc.tensor.matmul(s_ps[n][a * SPAN:(a + 1) * SPAN, col:col + queries],
                                                    xtT[h][:, key:key + SPAN], zT[h][:, key:key + queries],
                                                    start=True, stop=True, tile_position=(0, a * SPAN))
                    if n == 1 and h == 1:
                        last = nc.tensor.matmul(s_ps[1][C - SPAN:C, REACH + C:2 * REACH], xtT[0][:, UTOK - SPAN:UTOK],
                                                zT[1][:, 0:SPAN], start=True, stop=True,
                                                tile_position=(0, C - SPAN))
                    last.then_inc(s_done, 1)

            def mix_tokens(i, h):
                u = 2 * i + h
                pe.wait_ge(sm_ready, 2 * u + 2)
                used(sxT_ready, u)
                if h:
                    pe.wait_ge(carry_ready, i + 1)
                for k in range(TILES):
                    queries = min(REACH, UTOK - k * C)
                    last = nc.tensor.matmul(sx_ps[:, k * C:k * C + queries], xt[h][:, k, :], sm[h][:, k, 0:queries],
                                            start=(k == 0), stop=(k == TILES - 1 and not h), skip_group_check=True)
                if h:
                    last = nc.tensor.matmul(sx_ps[:, 0:SPAN], xt_carry[:, :], sm[h][:, TILES - 1, C:REACH],
                                            start=False, stop=True, skip_group_check=True)
                last.then_inc(sx_done, 1)

            def attention_out(i, h, tiles=range(TILES)):
                u = 2 * i + h
                if tiles[0] == 0:
                    pe.wait_ge(sxT_ready, u + 1)
                    used(att_ready, u - 1)
                for k in tiles:
                    last = nc.tensor.matmul(o_ps[h][:, k * C:(k + 1) * C], sxT[h][:, k * C:(k + 1) * C], wv_sb[:, :],
                                            start=True, stop=True)
                if k == TILES - 1:
                    last.then_inc(o_done, 1)

            def ffn(i, h, tiles=range(TILES)):
                u = 2 * i + h
                if tiles[0] == 0:
                    used(xy_ready, u)
                for k in tiles:
                    last = nc.tensor.matmul(y_ps[:, k * C:(k + 1) * C], xtT[h][:, k * C:(k + 1) * C], wf_sb[:, :],
                                            start=True, stop=True)
                if k == TILES - 1:
                    last.then_inc(y_done, 1)

            def keep_busy(count, bank):
                for _ in range(count):
                    nc.tensor.matmul(bank[:, 0:C], ones[:, :], ones[:, :], start=True, stop=True)

            pe.wait_ge(ones_set, 1)
            keep_busy(WARM, o_ps[0])
            pe.wait_ge(centre_set, 1)
            pe.wait_ge(wqkv_in, 16)
            for n in range(3):
                nc.tensor.matmul(qkvT_ps[n][:, 0:C], wqkv_sb[:, n * C:(n + 1) * C], centre[:, :],
                                 start=True, stop=True).then_inc(qkvT_done, 1)
                if n == 0:
                    pe.wait_ge(bqkv_in, 16)
                    pe.wait_ge(ident_set, 1)
                    nc.tensor.matmul(z_ps[:, 0:3], bqkv_rows[:, :], ident[0:3, 0:3],
                                     start=True, stop=True).then_inc(bias_done, 1)
            pe.wait_ge(dmax_ready, 1)
            nc.tensor.matmul(sx_ps[:, 0:C], ones[:, :], dmax[:, :], start=True, stop=True).then_inc(gmax_done, 1)
            pe.wait_ge(qkvT_ready, 2)
            nc.tensor.matmul(z_ps[:, 0:C], qkvT[:, 0:C], qkvT[:, C:2 * C], start=True, stop=True).then_inc(g_done, 1)
            pe.wait_ge(ident_set, 1)
            pe.wait_ge(xt_head_ready, 1)
            pe.wait_ge(xt_tail_ready, 1)
            for n in range(2):
                for k in range(HALFU):
                    last = nc.tensor.transpose(first_xT[n][:, k * C:(k + 1) * C], xt[0][:, n * HALFU + k, :],
                                               ident[:, :])
                last.then_inc(half_xT_done[n], 1)
            pe.wait_ge(qkvT_ready, 3)
            nc.tensor.matmul(o_ps[0][:, 0:C], qkvT[:, 2 * C:3 * C], centre[:, :],
                             start=True, stop=True).then_inc(wv_done, 1)
            pe.wait_ge(a_in, 16)
            nc.tensor.matmul(y_ps[0:RANK, 0:C], a_sb[:, :], centre[:, :], start=True, stop=True).then_inc(aT_done, 1)
            pe.wait_ge(g_ready, 1)
            pe.wait_ge(dve_chain, 2)
            for n in range(2):
                pe.wait_ge(half_xtT_ready[n], 1)
                nc.tensor.matmul(first_z[n][:, 0:HTOK], g_sb[:, :], xtT[0][:, n * HTOK:(n + 1) * HTOK],
                                 start=True, stop=True).then_inc(half_z_done[n], 1)
            transpose_unit(0, 1)
            pe.wait_ge(s_ps_zeroed, 1)
            scores(0, 0)

            project_z(0, 1)
            pe.wait_ge(aT_ready, 1)
            pe.wait_ge(b_in, 16)
            nc.tensor.matmul(w_ps[:, 0:C], aT_sb[:, :], b_sb[:, :], start=True, stop=False)
            mix_tokens(0, 0)
            scores(0, 1)
            pe.wait_ge(biasf_in, 16)
            pe.wait_ge(lnb_in, 16)
            nc.tensor.matmul(w_ps[:, 0:C], inv_rows[:, :], bias_rows[:, :], start=False, stop=False)
            pe.wait_ge(wv_ready, 1)
            attention_out(0, 0, range(TILES - 1))
            pe.wait_ge(wq4_ready, 1)
            nc.tensor.matmul(w_ps[:, 0:C], centre[:, :], wq4[:, :], start=False, stop=True).then_inc(wf_done, 1)
            attention_out(0, 0, range(TILES - 1, TILES))
            transpose_unit(1, 0)
            pe.wait_ge(wf_ready, 1)
            ffn(0, 0)

            def step(i, h, following, transposed=False):
                if not transposed:
                    transpose_unit(*following)
                mix_tokens(i, h)
                project_z(*following)
                ffn(i, h, range(EARLY))
                attention_out(i, h)
                scores(*following)
                ffn(i, h, range(EARLY, TILES))

            step(0, 1, (1, 0), transposed=True)
            with pe.Fori(0, B - 2) as i:
                step(i + 1, 0, (i + 1, 1))
                step(i + 1, 1, (i + 2, 0))
            step(B - 1, 0, (B - 1, 1))
            pe.wait_ge(sm_ready, 4 * B)
            pe.wait_ge(carry_ready, B)
            pe.wait_ge(sxT_ready, 2 * B - 1)
            pe.wait_ge(zT_ready, 2 * B)
            for n in range(2):
                first = n * HALFU
                spill = xt_carry[:, :] if n == 0 else xt[1][:, first - 1, :]
                spill_tile = (first - 1) % TILES
                nc.tensor.matmul(last_sx[n][:, 0:REACH], xt[1][:, first, :], sm[1][:, first, :],
                                 start=True, stop=False, skip_group_check=True)
                nc.tensor.matmul(last_sx[n][:, 0:SPAN], spill, sm[1][:, spill_tile, C:REACH],
                                 start=False, stop=False, skip_group_check=True)
                nc.tensor.matmul(last_sx[n][:, C:HTOK], xt[1][:, first + 1, :], sm[1][:, first + 1, 0:C],
                                 start=False, stop=True, skip_group_check=True).then_inc(half_sx_done, 1)
            pe.wait_ge(att_ready, 2 * B - 2)
            pe.wait_ge(xy_ready, 2 * B - 1)

            def last_attention(n):
                pe.wait_ge(half_sxT_ready, n + 1)
                for k in range(HALFU):
                    col = n * HTOK + k * C
                    last = nc.tensor.matmul(last_o[n][:, k * C:(k + 1) * C], sxT[1][:, col:col + C], wv_sb[:, :],
                                            start=True, stop=True)
                last.then_inc(half_o_done, 1)

            def last_ffn(tile):
                n, k = divmod(tile, HALFU)
                nc.tensor.matmul(last_y[n][:, k * C:(k + 1) * C], xtT[1][:, tile * C:(tile + 1) * C], wf_sb[:, :],
                                 start=True, stop=False)

            def last_residual(tile):
                n, k = divmod(tile, HALFU)
                cols = slice(k * C, (k + 1) * C)
                last = nc.tensor.matmul(last_y[n][:, cols], ident[:, :], x_sb[:, (2 * B - 1) * TILES + tile, :],
                                        start=False, stop=True)
                if k == HALFU - 1:
                    last.then_inc(half_y_done, 1)

            last_attention(0)
            last_ffn(0)
            last_attention(1)
            last_residual(0)
            for tile in range(1, TILES):
                last_ffn(tile)
                last_residual(tile)


_INS = ['L0_attn_x', 'L0_attn_W_qkv', 'L0_attn_b_qkv', 'L0_attn_ln_w', 'L0_attn_ln_b',
        'L0_ffn_kernel', 'L0_ffn_bias', 'L0_ffn_a', 'L0_ffn_b']
_OUTS = [((4, 1024, 128), 'float32')]


def kernel(**inputs):
    import numpy as _np
    import concourse.bacc as _bacc
    from concourse import mybir as _mybir
    from concourse.bass_utils import run_bass_kernel_spmd as _run

    nc = _bacc.Bacc("TRN2", target_bir_lowering=False, num_devices=1)
    arrays, args = {}, []
    for name in _INS:
        a = _np.ascontiguousarray(inputs[name])
        arrays[f"in_{name}_dram"] = a
        args.append(nc.dram_tensor(f"in_{name}_dram", a.shape, _mybir.dt.from_np(a.dtype), kind="ExternalInput").ap())
    for i, (shape, dtype) in enumerate(_OUTS):
        dt = _mybir.dt.from_np(_np.dtype(dtype))
        args.append(nc.dram_tensor(f"out_{i}_dram", shape, dt, kind="ExternalOutput").ap())
    band_block_kernel(nc, *args)
    r = _run(nc, [arrays], core_ids=[0])
    got = tuple(r.results[0][f"out_{i}_dram"] for i in range(len(_OUTS)))
    return got[0]
```
